# Optimizing a Trainium2 kernel written in Bass

```python
import numpy as np
import jax
import jax.numpy as jnp

def _softmax(x, axis=-1):
    return jax.nn.softmax(x, axis=axis)

def _gelu(x):
    return jax.nn.gelu(x, approximate=True)

def _silu(x):
    return jax.nn.silu(x)

def _sigmoid(x):
    return jax.nn.sigmoid(x)

def _layernorm(x, axis=-1, eps=1e-05):
    m = jnp.mean(x, axis=axis, keepdims=True)
    v = jnp.var(x, axis=axis, keepdims=True)
    return (x - m) / jnp.sqrt(v + eps)

def _scatter_add(tgt, idx, src, axis=0):
    return tgt.at[idx].add(src)

def _segment_sum(src, seg, n):
    return jax.ops.segment_sum(src, seg, n)
kernel_name = 'mk_adaln_d2_jaxref_r8_17059a'

def setup_inputs(seed: int=0):
    np.random.seed(seed)
    _w = jnp.asarray

    def _L0_attn_setup():
        import jax, jax.numpy as jnp
        import numpy as np
        import math
        B, S, D_IN, D_KQ, D_OUT = (4, 256, 128, 128, 128)
        key = jax.random.key(seed)
        ks = jax.random.split(key, 7)
        sc = 0.02
        return {'x': jax.random.normal(ks[0], (B, S, D_IN), jnp.float32), 'Wq': jax.random.normal(ks[1], (D_KQ, D_IN), jnp.float32) * sc, 'bq': jax.random.normal(ks[2], (D_KQ,), jnp.float32) * sc, 'Wk': jax.random.normal(ks[3], (D_KQ, D_IN), jnp.float32) * sc, 'bk': jax.random.normal(ks[4], (D_KQ,), jnp.float32) * sc, 'Wv': jax.random.normal(ks[5], (D_OUT, D_IN), jnp.float32) * sc, 'bv': jax.random.normal(ks[6], (D_OUT,), jnp.float32) * sc}
    _L0_attn_in = _L0_attn_setup()

    def _L0_ffn_setup():
        import math
        import jax, jax.numpy as jnp
        import numpy as np
        NUM_EXPERTS = 8
        CAPACITY_FACTOR = 1.5
        key = jax.random.key(seed)
        ks = jax.random.split(key, 4)
        B, T, D, F, E = (4, 256, 128, 512, NUM_EXPERTS)
        scale = 0.02
        return {'x': jax.random.normal(ks[0], (B, T, D), dtype=jnp.float32), 'router_w': jax.random.normal(ks[1], (E, D), dtype=jnp.float32) * scale, 'w1': jax.random.normal(ks[2], (E, D, F), dtype=jnp.float32) * scale, 'b1': jnp.zeros((E, F), dtype=jnp.float32), 'w2': jax.random.normal(ks[3], (E, F, D), dtype=jnp.float32) * scale, 'b2': jnp.zeros((E, D), dtype=jnp.float32)}
    _L0_ffn_in = _L0_ffn_setup()
    _L0_c = _w((lambda *s: np.random.randn(*s).astype(np.float32) * 0.05)(2, 128))
    _L0_wmod = _w((lambda *s: np.random.randn(*s).astype(np.float32) * 0.05)(128, 6 * 128) * 128 ** (-0.5))

    def _L1_attn_setup():
        import math
        import jax, jax.numpy as jnp
        import numpy as np
        N_HEADS = 16
        D_KV = 64
        NUM_BUCKETS = 32
        MAX_DISTANCE = 128

        def _relative_position_bucket(relative_position, num_buckets=NUM_BUCKETS, max_distance=MAX_DISTANCE):
            num_buckets //= 2
            n = -relative_position
            ret = (n < 0).astype(jnp.int32) * num_buckets
            n = jnp.abs(n)
            max_exact = num_buckets // 2
            is_small = n < max_exact
            val_if_large = max_exact + (jnp.log(jnp.maximum(n, 1).astype(jnp.float32) / max_exact) / math.log(max_distance / max_exact) * (num_buckets - max_exact)).astype(jnp.int32)
            val_if_large = jnp.minimum(val_if_large, num_buckets - 1)
            return ret + jnp.where(is_small, n, val_if_large)
        key = jax.random.key(seed)
        ks = jax.random.split(key, 6)
        B, S, D = (2, 256, 128)
        scale = 0.02
        return {'x': jax.random.normal(ks[0], (B, S, D), dtype=jnp.float32), 'Wq': jax.random.normal(ks[1], (D, N_HEADS * D_KV), dtype=jnp.float32) * scale, 'Wk': jax.random.normal(ks[2], (D, N_HEADS * D_KV), dtype=jnp.float32) * scale, 'Wv': jax.random.normal(ks[3], (D, N_HEADS * D_KV), dtype=jnp.float32) * scale, 'Wo': jax.random.normal(ks[4], (N_HEADS * D_KV, D), dtype=jnp.float32) * scale, 'rel_emb': jax.random.normal(ks[5], (NUM_BUCKETS, N_HEADS), dtype=jnp.float32) * scale}
    _L1_attn_in = _L1_attn_setup()

    def _L1_ffn_setup():
        import jax, jax.numpy as jnp
        import numpy as np
        B, S, D_MODEL, D_FF, E, R, TOP_K = (4, 256, 128, 512, 8, 16, 2)
        key = jax.random.key(seed)
        ks = jax.random.split(key, 9)
        sd = 1.0 / np.sqrt(D_MODEL)
        return {'hidden_states': jax.random.normal(ks[0], (B, S, D_MODEL), jnp.float32), 'wi': jax.random.normal(ks[1], (D_FF, D_MODEL), jnp.float32) * sd, 'bi': jax.random.normal(ks[2], (D_FF,), jnp.float32) * 0.01, 'wo': jax.random.normal(ks[3], (D_MODEL, D_FF), jnp.float32) * (1.0 / np.sqrt(D_FF)), 'bo': jax.random.normal(ks[4], (D_MODEL,), jnp.float32) * 0.01, 'lora_A': jax.random.normal(ks[5], (E, R, D_MODEL), jnp.float32) * sd, 'lora_B': jax.random.normal(ks[6], (E, D_FF, R), jnp.float32) * 0.02, 'gate_w': jax.random.normal(ks[7], (E, D_MODEL), jnp.float32) * sd, 'gate_b': jax.random.normal(ks[8], (E,), jnp.float32) * 0.01}
    _L1_ffn_in = _L1_ffn_setup()
    _L1_c = _w((lambda *s: np.random.randn(*s).astype(np.float32) * 0.05)(2, 128))
    _L1_wmod = _w((lambda *s: np.random.randn(*s).astype(np.float32) * 0.05)(128, 6 * 128) * 128 ** (-0.5))
    _d = {'L0_attn_x': _L0_attn_in['x'], 'L0_attn_Wq': _L0_attn_in['Wq'], 'L0_attn_bq': _L0_attn_in['bq'], 'L0_attn_Wk': _L0_attn_in['Wk'], 'L0_attn_bk': _L0_attn_in['bk'], 'L0_attn_Wv': _L0_attn_in['Wv'], 'L0_attn_bv': _L0_attn_in['bv'], 'L0_ffn_router_w': _L0_ffn_in['router_w'], 'L0_ffn_w1': _L0_ffn_in['w1'], 'L0_ffn_b1': _L0_ffn_in['b1'], 'L0_ffn_w2': _L0_ffn_in['w2'], 'L0_ffn_b2': _L0_ffn_in['b2'], 'L0_c': _L0_c, 'L0_wmod': _L0_wmod, 'L1_attn_Wq': _L1_attn_in['Wq'], 'L1_attn_Wk': _L1_attn_in['Wk'], 'L1_attn_Wv': _L1_attn_in['Wv'], 'L1_attn_Wo': _L1_attn_in['Wo'], 'L1_attn_rel_emb': _L1_attn_in['rel_emb'], 'L1_ffn_wi': _L1_ffn_in['wi'], 'L1_ffn_bi': _L1_ffn_in['bi'], 'L1_ffn_wo': _L1_ffn_in['wo'], 'L1_ffn_bo': _L1_ffn_in['bo'], 'L1_ffn_lora_A': _L1_ffn_in['lora_A'], 'L1_ffn_lora_B': _L1_ffn_in['lora_B'], 'L1_ffn_gate_w': _L1_ffn_in['gate_w'], 'L1_ffn_gate_b': _L1_ffn_in['gate_b'], 'L1_c': _L1_c, 'L1_wmod': _L1_wmod}
    _x0 = _d['L0_attn_x']
    _d['L0_attn_x'] = jax.random.normal(jax.random.fold_in(jax.random.key(seed), 1), (2, 1024, 128), dtype=_x0.dtype)
    del _x0
    return _d

def reference(L0_attn_x, L0_attn_Wq, L0_attn_bq, L0_attn_Wk, L0_attn_bk, L0_attn_Wv, L0_attn_bv, L0_ffn_router_w, L0_ffn_w1, L0_ffn_b1, L0_ffn_w2, L0_ffn_b2, L0_c, L0_wmod, L1_attn_Wq, L1_attn_Wk, L1_attn_Wv, L1_attn_Wo, L1_attn_rel_emb, L1_ffn_wi, L1_ffn_bi, L1_ffn_wo, L1_ffn_bo, L1_ffn_lora_A, L1_ffn_lora_B, L1_ffn_gate_w, L1_ffn_gate_b, L1_c, L1_wmod):

    def _L0_attn_ref(x, Wq, bq, Wk, bk, Wv, bv):
        import jax, jax.numpy as jnp
        import numpy as np
        import math
        B, S, D_IN, D_KQ, D_OUT = (4, 256, 128, 128, 128)
        Q = jnp.einsum('bsd,kd->bsk', x, Wq) + bq
        K = jnp.einsum('bsd,kd->bsk', x, Wk) + bk
        V = jnp.einsum('bsd,od->bso', x, Wv) + bv
        scale = 1.0 / math.sqrt(D_KQ)
        attn = jnp.einsum('bqk,bsk->bqs', Q, K) * scale
        s = attn.shape[-1]
        causal = jnp.tril(jnp.ones((s, s), dtype=bool))
        attn = jnp.where(causal[None, :, :], attn, -jnp.inf)
        attn = jax.nn.softmax(attn, axis=-1)
        Z = jnp.einsum('bqs,bso->bqo', attn, V)
        return Z

    def _L0_ffn_ref(x, router_w, w1, b1, w2, b2):
        import math
        import jax, jax.numpy as jnp
        import numpy as np
        NUM_EXPERTS = 8
        CAPACITY_FACTOR = 1.5
        B, T, D = x.shape
        E = router_w.shape[0]
        N = B * T
        C = max(math.ceil(CAPACITY_FACTOR * N / E), 1)
        x_flat = x.reshape(N, D)
        logits = x_flat @ router_w.T
        probs = jax.nn.softmax(logits, axis=-1)
        chosen_e = jnp.argmax(probs, axis=-1)
        chosen_p = jnp.max(probs, axis=-1)
        onehot = jax.nn.one_hot(chosen_e, E, dtype=jnp.float32)
        pos = jnp.take_along_axis(jnp.cumsum(onehot, axis=0), chosen_e[:, None], axis=1)[:, 0] - 1.0
        pos = pos.astype(jnp.int32)
        kept = pos < C
        pos_c = jnp.clip(pos, 0, C - 1)
        buf = jnp.zeros((E, C, D), dtype=x.dtype).at[chosen_e, pos_c].add(x_flat * kept[:, None].astype(x.dtype))
        h = jax.nn.gelu(jnp.einsum('ecd,edf->ecf', buf, w1) + b1[:, None, :], approximate=False)
        eo = jnp.einsum('ecf,efd->ecd', h, w2) + b2[:, None, :]
        y = eo[chosen_e, pos_c] * (chosen_p * kept.astype(x.dtype))[:, None]
        return y.reshape(B, T, D)

    def _L1_attn_ref(x, Wq, Wk, Wv, Wo, rel_emb):
        import math
        import jax, jax.numpy as jnp
        import numpy as np
        N_HEADS = 16
        D_KV = 64
        NUM_BUCKETS = 32
        MAX_DISTANCE = 128

        def _relative_position_bucket(relative_position, num_buckets=NUM_BUCKETS, max_distance=MAX_DISTANCE):
            num_buckets //= 2
            n = -relative_position
            ret = (n < 0).astype(jnp.int32) * num_buckets
            n = jnp.abs(n)
            max_exact = num_buckets // 2
            is_small = n < max_exact
            val_if_large = max_exact + (jnp.log(jnp.maximum(n, 1).astype(jnp.float32) / max_exact) / math.log(max_distance / max_exact) * (num_buckets - max_exact)).astype(jnp.int32)
            val_if_large = jnp.minimum(val_if_large, num_buckets - 1)
            return ret + jnp.where(is_small, n, val_if_large)
        B, S, D = x.shape
        H, Dk = (N_HEADS, D_KV)

        def shape(t):
            return t.reshape(B, S, H, Dk).transpose(0, 2, 1, 3)
        q = shape(x @ Wq)
        k = shape(x @ Wk)
        v = shape(x @ Wv)
        scores = jnp.einsum('bhqd,bhkd->bhqk', q, k)
        ctx_pos = jnp.arange(S)[:, None]
        mem_pos = jnp.arange(S)[None, :]
        rp_bucket = _relative_position_bucket(mem_pos - ctx_pos)
        position_bias = rel_emb[rp_bucket].transpose(2, 0, 1)[None]
        weights = jax.nn.softmax(scores + position_bias, axis=-1)
        context = jnp.einsum('bhqk,bhkd->bhqd', weights, v)
        context = context.transpose(0, 2, 1, 3).reshape(B, S, H * Dk)
        return context @ Wo

    def _L1_ffn_ref(hidden_states, wi, bi, wo, bo, lora_A, lora_B, gate_w, gate_b):
        import jax, jax.numpy as jnp
        import numpy as np
        B, S, D_MODEL, D_FF, E, R, TOP_K = (4, 256, 128, 512, 8, 16, 2)
        logits = jnp.einsum('bsd,ed->bse', hidden_states, gate_w) + gate_b
        scores = jax.nn.softmax(logits, axis=-1)
        top_v, top_i = jax.lax.top_k(scores, TOP_K)
        val_sum = top_v.sum(axis=-1)
        out = jnp.zeros_like(hidden_states)
        for e in range(E):
            count = (top_i == e).sum(axis=-1).astype(hidden_states.dtype)
            gate = count * val_sum
            inter = jnp.einsum('bsd,fd->bsf', hidden_states, wi) + bi + jnp.einsum('bsr,fr->bsf', jnp.einsum('bsd,rd->bsr', hidden_states, lora_A[e]), lora_B[e])
            h = jax.nn.relu(inter)
            expert_out = jnp.einsum('bsf,df->bsd', h, wo) + bo
            out = out + gate[..., None] * expert_out
        return out
    x = L0_attn_x
    mod = (_silu(L0_c) @ L0_wmod).reshape(L0_c.shape[0], 6, 1, -1)
    sa, ca, ga, sb, cb, gb = (mod[:, 0], mod[:, 1], mod[:, 2], mod[:, 3], mod[:, 4], mod[:, 5])
    ga = (2 * (ga >= 0) - 1) * jnp.maximum(jnp.abs(ga), 0.25)
    gb = (2 * (gb >= 0) - 1) * jnp.maximum(jnp.abs(gb), 0.25)
    h = _layernorm(x, axis=-1) * (1 + ca) + sa
    x = x + ga * _L0_attn_ref(h, L0_attn_Wq, L0_attn_bq, L0_attn_Wk, L0_attn_bk, L0_attn_Wv, L0_attn_bv)
    h = _layernorm(x, axis=-1) * (1 + cb) + sb
    x = x + gb * _L0_ffn_ref(h, L0_ffn_router_w, L0_ffn_w1, L0_ffn_b1, L0_ffn_w2, L0_ffn_b2)
    mod = (_silu(L1_c) @ L1_wmod).reshape(L1_c.shape[0], 6, 1, -1)
    sa, ca, ga, sb, cb, gb = (mod[:, 0], mod[:, 1], mod[:, 2], mod[:, 3], mod[:, 4], mod[:, 5])
    ga = (2 * (ga >= 0) - 1) * jnp.maximum(jnp.abs(ga), 0.25)
    gb = (2 * (gb >= 0) - 1) * jnp.maximum(jnp.abs(gb), 0.25)
    h = _layernorm(x, axis=-1) * (1 + ca) + sa
    x = x + ga * _L1_attn_ref(h, L1_attn_Wq, L1_attn_Wk, L1_attn_Wv, L1_attn_Wo, L1_attn_rel_emb)
    h = _layernorm(x, axis=-1) * (1 + cb) + sb
    x = x + gb * _L1_ffn_ref(h, L1_ffn_wi, L1_ffn_bi, L1_ffn_wo, L1_ffn_bo, L1_ffn_lora_A, L1_ffn_lora_B, L1_ffn_gate_w, L1_ffn_gate_b)
    return x

_drawn_inputs = setup_inputs


def setup_inputs(seed=0):
    import zlib

    import numpy as np

    out = dict(_drawn_inputs(seed))
    spreads = {'L0_ffn_b1': (0.0, 0.8), 'L0_ffn_b2': (0.0, 0.8)}
    factors = {'L0_attn_Wq': 8.0,
     'L0_attn_bq': 8.0,
     'L0_attn_Wk': 8.0,
     'L0_attn_bk': 64.0,
     'L0_attn_Wv': 8.0,
     'L0_attn_bv': 8.0,
     'L0_ffn_router_w': 8.0,
     'L0_ffn_w1': 8.0,
     'L0_ffn_w2': 8.0,
     'L0_c': 6.61,
     'L0_wmod': 6.561,
     'L1_attn_Wq': 8.0,
     'L1_attn_Wk': 8.0,
     'L1_attn_Wv': 8.0,
     'L1_attn_Wo': 8.0,
     'L1_attn_rel_emb': 22.083,
     'L1_ffn_bi': 64.0,
     'L1_ffn_bo': 49.956,
     'L1_ffn_lora_A': 5.261,
     'L1_ffn_lora_B': 5.237,
     'L1_ffn_gate_b': 8.0}
    for name, (base, spread) in spreads.items():
        noise = np.random.default_rng([zlib.crc32(name.encode()), seed]).standard_normal(out[name].shape)
        drawn = base * np.exp(spread * noise) if base else spread * noise
        out[name] = jnp.asarray(drawn.astype(out[name].dtype))
    for name, factor in factors.items():
        out[name] = (out[name] * factor).astype(out[name].dtype)
    return out
```

```python
from contextlib import ExitStack

import numpy as np

import concourse.bass as bass
from concourse import mybir

F32 = mybir.dt.float32
F32R = mybir.dt.float32r
BF16 = mybir.dt.bfloat16
U32 = mybir.dt.uint32
ALU = mybir.AluOpType
ACT = mybir.ActivationFunctionType
AX = mybir.AxisListType

P = 128
B, S, D = 2, 1024, 128
TB = S // P
NT = B * TB
E = 8
F = 512
FC = F // P
N = B * S
CAP = -(-3 * N // (2 * E))
CT = CAP // P
H, DK = 16, 64
PAIRS = H // 2
R = 16
BUCKETS = 32
EPS = 1e-5
QK_SCALE = float(D) ** -0.5
NEG = -3.0e38
VEC = 2048
STRIP = S + (TB - 1) * P
CK = 512
STEPS = 4 * TB
UNIT = 2 * TB
ROWS = 64


def rel_one_hot():
    hot = np.zeros((BUCKETS, VEC), np.float32)
    for col in range(VEC - 1):
        rel = col - (S - 1)
        n = abs(rel)
        if n < 8:
            bucket = n
        else:
            bucket = min(8 + (n * n // 64).bit_length() - 1, 15)
        hot[bucket + (16 if rel > 0 else 0), col] = 1.0
    return hot


def build(nc, rel_hot, L0_attn_x, L0_attn_Wq, L0_attn_bq, L0_attn_Wk, L0_attn_bk, L0_attn_Wv, L0_attn_bv,
          L0_ffn_router_w, L0_ffn_w1, L0_ffn_b1, L0_ffn_w2, L0_ffn_b2, L0_c, L0_wmod,
          L1_attn_Wq, L1_attn_Wk, L1_attn_Wv, L1_attn_Wo, L1_attn_rel_emb,
          L1_ffn_wi, L1_ffn_bi, L1_ffn_wo, L1_ffn_bo, L1_ffn_lora_A, L1_ffn_lora_B,
          L1_ffn_gate_w, L1_ffn_gate_b, L1_c, L1_wmod, out):
    with ExitStack() as ctx:
        ctx.enter_context(nc.allow_non_contiguous_dma(reason="small weight rearrangements"))

        def sb(name, shape, dt=F32):
            return ctx.enter_context(nc.sbuf_tensor(name, shape, dt))

        def ps(name, cols):
            return ctx.enter_context(nc.psum_tensor(name, [P, cols], F32))

        def sem(name):
            return ctx.enter_context(nc.semaphore(name))

        slots_in = nc.dram_tensor("slots_in", (E * CAP + N, D), F32, kind="Internal").ap()
        slots_out = nc.dram_tensor("slots_out", (E * CAP, D), F32, kind="Internal").ap()
        bias_vec = nc.dram_tensor("bias_vec", (H, VEC), F32, kind="Internal")

        x = sb("x", [P, NT, D])
        hT = sb("hT", [P, N])
        ident = sb("ident", [P, P])
        mod = sb("mod", [P, B, 6, D])
        cols = sb("cols", [P, ROWS])
        probs = sb("probs", [P, 2, S])
        probsT = sb("probsT", [P, 2, 2, TB, P])
        QS = sb("QS", [P, 2, 2, S], F32R)
        KS = sb("KS", [P, 2, 2, 2, S], F32R)
        stage = sb("stage", [P, 4, CK], F32R)
        V1 = sb("V1", [P, 2, TB, P])
        wpair = sb("wpair", [P, 3, P])
        strips = sb("strips", [P, 2, 2, STRIP])
        arena = sb("arena", [P, PAIRS * N])
        Rsb = sb("Rsb", [P, 2, P])
        nmax = sb("nmax", [P, 4])
        rsum = sb("rsum", [P, 8])
        rinv = sb("rinv", [P, 4])
        rwide = sb("rwide", [P, 2, 2, DK])
        st = sb("st", [P, 8, NT])
        iota8 = st[:, 1, 0:E]

        ctxT = arena[:, :].rearrange("p (a n) -> p a n", a=PAIRS)

        def part(region, at, n):
            return region[:, at:at + n]

        w1 = part(arena, 0, E * F).rearrange("p (e f) -> p e f", e=E)
        w2 = part(arena, 4096, E * F).rearrange("p (e c d) -> p e c d", e=E, c=FC)
        slotT = part(arena, 8192, E * CAP)
        slot_rows = part(arena, 11264, E * CAP).rearrange("p (t d) -> p t d", t=E * CT)
        wmod = [part(arena, 14336, 768), part(arena, 15104, 768)]
        siluT = part(arena, 15872, 4)
        before = part(arena, 15876, 64).bitcast(BF16)
        ones = part(arena, 15940, 64).bitcast(BF16)
        hot1b = part(arena, 16004, 68).bitcast(BF16).rearrange("p (t e) -> p t e", e=E)
        slot_s = part(arena, 16072, NT).bitcast(U32)
        slot_g = part(arena, 16088, NT).bitcast(U32)
        iota_n = part(arena, 16104, NT)
        iota_c = part(arena, 16120, E)
        flat = strips[:, :, :, :].rearrange("p a h n -> p (a h n)")
        q0T, k0T = part(flat, 0, N), part(flat, N, N)
        v0 = part(flat, 2 * N, N).rearrange("p (t d) -> p t d", t=NT)
        w0raw = part(flat, 3 * N, 384).rearrange("p (w d) -> p w d", w=3)
        w0T = part(flat, 3 * N + 384, 384).rearrange("p (w d) -> p w d", w=3)
        bvb = part(flat, 3 * N + 768, D)
        raw = part(flat, 0, 13 * P).rearrange("p (w d) -> p w d", w=13)
        wT = part(flat, 13 * P, 13 * P).rearrange("p (w d) -> p w d", w=13)
        bob = part(flat, 26 * P, D)
        gbb = part(flat, 27 * P, E)
        woall = part(flat, 28 * P, PAIRS * D).rearrange("p (a d) -> p a d", a=PAIRS)
        lowrank = part(flat, 36 * P, 4 * P)
        masked = part(flat, 40 * P, 8 * P).rearrange("p (j n) -> p j n", j=2)
        hot_wide = part(flat, 0, 8 * P).rearrange("p (j t d) -> p j t d", j=2, t=4)
        h = probs[:, :, :].rearrange("p a (t d) -> p (a t) d", d=D)
        tmp = probsT[:, :, :, :, :].rearrange("p a h k q -> p (a h k) q")
        tmp1, tmp2 = tmp[:, 0:NT, :], tmp[:, NT:2 * NT, :]
        gelu = tmp[:, 0:24, :].rearrange("p (a c t) q -> p a c (t q)", a=2, c=FC)
        act_r = tmp.rearrange("p (a c t) q -> p a c (t q)", a=2, c=FC)
        b2b = V1[:, 0, :, :]
        rt = V1[:, 1, 1:7, :].rearrange("p a (t e) -> p a t e", e=E)
        causal = V1[:, 1, 7, :]
        rows = V1[0:ROWS, 1, 0, :]
        vec_sb = arena[0:H, 8192:8192 + VEC]
        hot_sb = arena[32:32 + BUCKETS, 8192:8192 + VEC]
        rel_sb = arena[32:32 + BUCKETS, 8192 + VEC:8192 + VEC + H]
        zero_rows = part(arena, 11264, E * CAP)

        SC = [ps("SC0", 2 * 512), ps("SC1", 2 * 512)]
        PT = [ps("PTA", 512), ps("PTB", 512)]
        CX = ps("CX", 512)
        MI = ps("MI", 512)
        CX0 = [CX[:, 0:P], MI[:, 0:P]]
        four = [PT[0][:, :], PT[1][:, :], CX[:, :], MI[:, :]]
        four_sc = [SC[0][:, 0:512], SC[0][:, 512:1024], SC[1][:, 0:512], SC[1][:, 512:1024]]

        sems = {}

        def ev(name):
            if name not in sems:
                sems[name] = ctx.enter_context(nc.semaphore("s_" + name))
            return sems[name]

        C_B1, C_BQ, C_BK, C_BI, C_C, C_RW, C_GW, NROWS = 0, 32, 33, 34, 38, 42, 50, 58
        WI, LA, WO, LB = 0, 4, 5, 9

        def bc_rows(ap, n):
            return ap.unsqueeze(2).to_broadcast([ap.shape[0], ap.shape[1], n])

        def bc_tiles(ap, n):
            return ap.unsqueeze(1).to_broadcast([ap.shape[0], n, ap.shape[1]])

        def tiles(b):
            return slice(b * TB, (b + 1) * TB)

        fills0 = [(kind, b, half) for b in range(B) for kind in "qkv" for half in range(2)]

        def out_of(f):
            mine = [g for g in range(f + 1) if (fills0[g][0] == "v") == (fills0[f][0] == "v")]
            return ("v0_out" if fills0[f][0] == "v" else "qk0_out"), len(mine)

        def load_strips(sp, copy, p):
            sp.dma_start(strips[:, copy, :, :],
                         bass.AP(bias_vec, p * (2 * VEC), [[1, P], [VEC, 2], [1, STRIP]])).then_inc(ev("strips%d" % copy), 16)

        def load_weights(sp, p):
            for n, w in enumerate((L1_attn_Wq, L1_attn_Wk, L1_attn_Wv)):
                sp.dma_start(wpair[:, n, :], w[:, bass.ts(p, P)]).then_inc(ev("ld_pair"), 16)

        def stack_half(sp, u, half):
            b, n = (u % 2, u) if isinstance(u, int) else (u[1], 2 * u[0] + u[1])
            for k in range(2):
                sp.wait_ge(ev("low_out"), 4 * n + 2 * half + k + 1)
                at = slice(half * 512, half * 512 + 512)
                for hd in range(2):
                    mine = slice(hd * DK, hd * DK + DK)
                    for part_ in range(2):
                        src = stage[mine, 2 * k + part_, :].bitcast(F32)
                        if k == 0:
                            sp.dma_start(QS[part_ * DK:part_ * DK + DK, b, hd, at].bitcast(F32), src).then_inc(ev("stacked_q"), 16)
                        else:
                            for copy in range(2):
                                sp.dma_start(KS[copy * DK:copy * DK + DK, b, hd, part_, at].bitcast(F32), src).then_inc(ev("stacked_k"), 16)

        def pair_dma(sp, p, last=False):
            sp.wait_ge(ev("scores"), STEPS * p)
            for half in range(2):
                stack_half(sp, (p, 1), half)
            if last:
                return
            sp.wait_ge(ev("proj_full"), 12 * p + 12)
            load_weights(sp, p + 1)
            sp.wait_ge(ev("nmax_done"), STEPS * p + UNIT)
            load_strips(sp, 0, p + 1)
            for half in range(2):
                stack_half(sp, (p + 1, 0), half)
            sp.wait_ge(ev("nmax_done"), STEPS * p + STEPS)
            load_strips(sp, 1, p + 1)

        chunks = [("q", 0), ("k", 0), ("q", 1), ("k", 1), ("v", 0), ("v", 1)]

        def has_chunk(i, last):
            return i < STEPS and i % 2 == 0 and i % UNIT < 12 and not (last and i >= UNIT)

        def act_chunk(act, u, c):
            b, n = (u % 2, u) if isinstance(u, int) else (u[1], 2 * u[0] + u[1])
            kind, q = chunks[c]
            act.wait_ge(ev("proj_full"), 6 * n + c + 1)
            if kind == "v":
                act.copy(V1[:, b, 4 * q:4 * q + 4, :].rearrange("p t d -> p (t d)"), MI[:, :]).then_inc(ev("high_out"), 1)
                return
            k = 0 if kind == "q" else 2
            if not (isinstance(u, int) and u == 0 and q == 0):
                act.wait_ge(ev("stacked_" + kind), (64 if kind == "q" else 128) * (2 * n + q))
            act.mul(stage[:, k, :], MI[:, :], -1.0 if kind == "q" else 1.0).then_inc(ev("high_out"), 1)

        def act_step(act, p, i, first=False, last=False):
            n = STEPS * p + i
            G = STEPS // 2
            if i % 2 == 0 and not (first and i < 4) and i < STEPS + 4:
                g = i // 2 - 2
                act.wait_ge(ev("r_full"), G * p + g + 1)
                if not (first and g < 2):
                    act.wait_ge(ev("ctx_out"), G * p + g - 1)
                act.copy(Rsb[:, g % 2, :], MI[:, 0:P]).then_inc(ev("r_out"), 1)
            if i < STEPS:
                act.wait_ge(ev("nmax_done"), n + 1)
                if not (first and i < 2):
                    act.wait_ge(ev("ptB_full"), n - 1)
                act.activation(probs[:, i % 2, :], SC[i % 2][:, :], ACT.Exp, bias=nmax[:, i % 4:i % 4 + 1],
                               scale=-1.0, accum_out=rsum[:, i % 4:i % 4 + 1]).then_inc(ev("exp_done"), 1)
            if not (first and i < 2) and i < STEPS + 2:
                j = (i - 2) % STEPS
                act.wait_ge(ev("ptA_full"), n - 1)
                if not (first and i < 6):
                    act.wait_ge(ev("pv_done"), G * p + (i - 2) // 2 - 1)
                act.copy(probsT[:, (j // 2) % 2, j % 2, 0:4, :].rearrange("p k q -> p (k q)"),
                         PT[0][:, :]).then_inc(ev("ptA_out"), 1)
            if has_chunk(i, last):
                act_chunk(act, (p + i // UNIT, (i // UNIT + 1) % 2), i % UNIT // 2)

        def pair_act(act, p, first=False, last=False):
            for i in range(STEPS):
                act_step(act, p, i, first, last)

        def dve_chunk(dve, u, c):
            n = u if isinstance(u, int) else 2 * u[0] + u[1]
            kind, q = chunks[c]
            if kind == "v":
                return
            k = 0 if kind == "q" else 2
            dve.wait_ge(ev("high_out"), 6 * n + c + 1)
            dve.scalar_tensor_tensor(out=stage[:, k + 1, :], in0=MI[:, :], scalar=-1.0 if kind == "q" else 1.0,
                                     in1=stage[:, k, :].bitcast(F32), op0=ALU.mult, op1=ALU.subtract).then_inc(ev("low_out"), 1)

        def dve_step(dve, p, i, first=False, last=False):
            n = STEPS * p + i
            if i % 2 == 0 and not (first and i < 6):
                g = i // 2 - 3
                dve.wait_ge(ev("r_out"), STEPS // 2 * p + g + 1)
                dve.wait_ge(ev("pv_done"), STEPS // 2 * p + g + 1)
                gg = g % (STEPS // 2)
                pair = p if g >= 0 else p - 1
                dve.tensor_tensor(arena[:, bass.ds(pair * N + gg * P, P)],
                                  bass.AP(CX, P - 1, [[512, P], [-1, P]]),
                                  bass.AP(Rsb, (g % 2) * P + P - 1, [[2 * P, P], [-1, P]]), ALU.mult).then_inc(ev("ctx_out"), 1)
            if i < STEPS:
                b, qt, hd = i // UNIT, (i % UNIT) // 2, i % 2
                dve.wait_ge(ev("scores"), n + 1)
                if i % UNIT == 0:
                    dve.wait_ge(ev("strips%d" % b), 16 * (p + 1) if isinstance(p, int) else p * 16 + 16)
                at = (TB - 1 - qt) * P
                dve.sem_inc(ev("minimum_started"), 1)
                dve.tensor_tensor_reduce(SC[hd][:, :], SC[hd][:, :], strips[:, b, hd, at:at + S], 1.0, 3.4e38,
                                         ALU.add, ALU.min, nmax[:, i % 4:i % 4 + 1]).then_inc(ev("nmax_done"), 1)
            if not (first and i < 2) and i < STEPS + 2:
                j = (i - 2) % STEPS
                dve.wait_ge(ev("ptB_full"), n - 1)
                if not (first and i < 6):
                    dve.wait_ge(ev("pv_done"), STEPS // 2 * p + (i - 2) // 2 - 1)
                dve.tensor_copy(probsT[:, (j // 2) % 2, j % 2, 4:8, :].rearrange("p k q -> p (k q)"),
                                PT[1][:, :]).then_inc(ev("ptB_out"), 1)
            if has_chunk(i, last):
                dve_chunk(dve, (p + i // UNIT, (i // UNIT + 1) % 2), i % UNIT // 2)
            if i % 2 == 0 and not (first and i < 2) and i < STEPS + 2:
                j = (i - 2) % 4
                dve.wait_ge(ev("exp_done"), n)
                if not (first and i < 6):
                    dve.wait_ge(ev("r_full"), STEPS // 2 * p + i // 2 - 2)
                dve.reciprocal(rwide[:, j // 2, :, :], rsum[:, j:j + 2].unsqueeze(2).to_broadcast([P, 2, DK])).then_inc(ev("rinv_done"), 1)

        def pair_dve(dve, p, first=False, last=False):
            for i in range(STEPS):
                dve_step(dve, p, i, first, last)

        def pe_chunk(pe, u, c):
            b, n = (u % 2, u) if isinstance(u, int) else (u[1], 2 * u[0] + u[1])
            kind, q = chunks[c]
            if c == 0 and b == 0:
                pe.wait_ge(ev("ld_pair"), (u[0] if not isinstance(u, int) else 0) * 48 + 48)
            if c >= 1 and chunks[c - 1][0] != "v":
                pe.wait_ge(ev("low_out"), 4 * n + c)
            elif not (isinstance(u, int) and u == 0 and c == 0):
                pe.wait_ge(ev("high_out"), 6 * n + c)
            at = b * S + q * CK
            if kind == "v":
                for t in range(4):
                    ins = pe.matmul(MI[:, t * P:(t + 1) * P], hT[:, at + t * P:at + (t + 1) * P], wpair[:, 2, :],
                                    start=True, stop=True)
            else:
                rhs = hT[:, at:at + CK]
                if kind == "q":
                    rhs = bass.AP(hT, at + P - 1, [[N, P], [P, CK // P], [-1, P]])
                ins = pe.matmul(MI[:, :], wpair[:, "qk".index(kind), :], rhs, start=True, stop=True)
            ins.then_inc(ev("proj_full"), 1)

        def pe_step(pe, p, i, first=False, last=False):
            n = STEPS * p + i
            G = STEPS // 2
            if i < STEPS:
                b, qt, hd = i // UNIT, (i % UNIT) // 2, i % 2
                if i % UNIT == 0:
                    pe.wait_ge(ev("stacked_q"), p * 256 + 128 * (b + 1))
                    pe.wait_ge(ev("stacked_k"), p * 512 + 256 * (b + 1))
                if not (first and i < 2):
                    pe.wait_ge(ev("exp_done"), n - 1)
                lhs = QS[:, b, hd, qt * P:(qt + 1) * P]
                for k in range(2):
                    for part_ in range(2):
                        ins = pe.matmul(SC[hd][:, k * 512:(k + 1) * 512], lhs, KS[:, b, hd, part_, k * 512:(k + 1) * 512],
                                        start=(part_ == 0), stop=(part_ == 1))
                ins.then_inc(ev("scores"), 1)
            if not (first and i < 2) and i < STEPS + 2:
                j = (i - 2) % STEPS
                pe.wait_ge(ev("exp_done"), n - 1)
                for half in range(2):
                    if not (first and i < 3):
                        pe.wait_ge(ev("ptA_out" if half == 0 else "ptB_out"), n - 2)
                    for t in range(4):
                        ins = pe.transpose(PT[half][:, t * P:(t + 1) * P],
                                           probs[:, j % 2, (4 * half + t) * P:(4 * half + t + 1) * P], ident[:, :])
                    ins.then_inc(ev("ptA_full" if half == 0 else "ptB_full"), 1)
            if has_chunk(i, last):
                if not (first and i < 4):
                    pe.wait_ge(ev("r_out"), G * p + i // 2 - 1)
                pe_chunk(pe, (p + i // UNIT, (i // UNIT + 1) % 2), i % UNIT // 2)
            if not (first and i < 4):
                g, half = i // 2 - 2, i % 2
                gg = g % G
                vb = gg // TB
                pe.wait_ge(ev("ptA_out" if half == 0 else "ptB_out"), STEPS * p + 2 * g + 2)
                if half == 0 and not (first and g < 1):
                    pe.wait_ge(ev("ctx_out"), G * p + g)
                for t in range(4 * half, 4 * half + 4):
                    for hd in range(2):
                        ins = pe.matmul(CX[hd * DK:(hd + 1) * DK, 0:P],
                                        V1[:, vb, t, hd * DK:(hd + 1) * DK], probsT[:, gg % 2, hd, t, :],
                                        start=(t == 0), stop=(t == TB - 1))
                if half == 1:
                    ins.then_inc(ev("pv_done"), 1)
            if i % 2 == 1 and not (first and i < 3) and i < STEPS + 3:
                g = (i - 3) // 2
                pe.wait_ge(ev("rinv_done"), G * p + g + 1)
                if has_chunk((i - 1) % STEPS if i < STEPS else STEPS, last):
                    c, n6 = (i % UNIT) // 2, 2 * p + i // UNIT + 1
                    if c < 4:
                        pe.wait_ge(ev("low_out"), 4 * n6 + c + 1)
                    else:
                        pe.wait_ge(ev("high_out"), 6 * n6 + c + 1)
                if not (first and g < 1):
                    pe.wait_ge(ev("r_out"), G * p + g)
                pe.transpose(MI[:, 0:P], rwide[:, g % 2, :, :].rearrange("p h d -> p (h d)"),
                             ident[:, :]).then_inc(ev("r_full"), 1)

        def pair_pe(pe, p, first=False, last=False):
            for i in range(STEPS):
                pe_step(pe, p, i, first, last)


        block = ctx.enter_context(nc.Block())

        @block.sync
        def _(sp):
            sp.dma_start(rows[C_B1:C_B1 + 32, :], L0_ffn_b1.rearrange("e (c f) -> (e c) f", c=FC)).then_inc(ev("ld_rows"), 16)
            sp.dma_start(rows[C_BQ:C_BQ + 1, :], L0_attn_bq.unsqueeze(0)).then_inc(ev("ld_rows"), 16)
            sp.dma_start(rows[C_BK:C_BK + 1, :], L0_attn_bk.unsqueeze(0)).then_inc(ev("ld_rows"), 16)
            sp.dma_start(rows[C_BI:C_BI + FC, :], L1_ffn_bi.rearrange("(c f) -> c f", c=FC)).then_inc(ev("ld_rows"), 16)
            sp.dma_start(rows[C_C:C_C + 2, :], L0_c).then_inc(ev("ld_rows"), 16)
            sp.dma_start(rows[C_C + 2:C_C + 4, :], L1_c).then_inc(ev("ld_rows"), 16)
            sp.dma_start(rows[C_RW:C_RW + E, :], L0_ffn_router_w).then_inc(ev("ld_rows"), 16)
            sp.dma_start(rows[C_GW:C_GW + E, :], L1_ffn_gate_w).then_inc(ev("ld_rows"), 16)
            for b in range(B):
                sp.dma_start(x[:, tiles(b), :], L0_attn_x[b].rearrange("(t p) d -> p t d", p=P)).then_inc(ev("ld_x%d" % b), 16)
            sp.dma_start(wmod[0], L0_wmod).then_inc(ev("ld_wmod"), 16)
            for n, w in enumerate((L0_attn_Wq, L0_attn_Wk, L0_attn_Wv)):
                sp.dma_start(w0raw[:, n, :], w).then_inc(ev("ld_w0"), 16)
            sp.dma_start(bvb, L0_attn_bv.unsqueeze(0).to_broadcast([P, D])).then_inc(ev("ld_bv"), 16)
            sp.dma_start(hot_sb, rel_hot).then_inc(ev("ld_rel"), 16)
            sp.dma_start(rel_sb, L1_attn_rel_emb).then_inc(ev("ld_rel"), 16)
            sp.dma_start(wmod[1], L1_wmod).then_inc(ev("ld_wmod1"), 16)
            sp.dma_start(w1, L0_ffn_w1.rearrange("e d f -> d e f")).then_inc(ev("ld_w1"), 16)
            sp.dma_start(w2, L0_ffn_w2.rearrange("e (c f) d -> f e c d", c=FC)).then_inc(ev("ld_w2"), 16)
            sp.dma_start(b2b, L0_ffn_b2.unsqueeze(0).to_broadcast([P, E, D])).then_inc(ev("ld_b2"), 16)
            sp.wait_ge(ev("zeros"), 1)
            sp.dma_start(slots_in[0:E * CAP, :].rearrange("(p r) d -> p (r d)", p=P), zero_rows).then_inc(ev("slots_zeroed"), 16)
            sp.wait_ge(ev("vec_ready"), 4)
            sp.dma_start(bias_vec.ap(), vec_sb).then_inc(ev("vec_stored"), 16)
            sp.wait_ge(ev("vec_stored"), 16)
            load_weights(sp, 0)
            sp.wait_ge(ev("scattered"), 16 * NT)
            sp.dma_start(slot_rows, slots_in[0:E * CAP, :].rearrange("(t p) d -> p t d", p=P)).then_inc(ev("slots_loaded"), 16)
            for e in range(E):
                sp.wait_ge(ev("expert_out"), e + 1)
                sp.dma_start(slots_out[e * CAP:(e + 1) * CAP, :].rearrange("(t p) d -> p t d", p=P),
                             slot_rows[:, e * CT:(e + 1) * CT, :]).then_inc(ev("slots_stored"), 16)
            load_strips(sp, 0, 0)
            load_strips(sp, 1, 0)
            for half in range(2):
                stack_half(sp, 0, half)
            pair_dma(sp, 0)
            with sp.Fori(1, PAIRS - 1) as p:
                pair_dma(sp, p)
            pair_dma(sp, PAIRS - 1, last=True)
            sp.wait_ge(ev("nmax_done"), STEPS * PAIRS)
            sp.dma_start(woall, L1_attn_Wo.rearrange("(a p) d -> p a d", p=P)).then_inc(ev("ld_wo"), 16)
            sp.dma_start(raw[:, WI:WI + FC, :], L1_ffn_wi.rearrange("(c p) d -> p c d", p=P)).then_inc(ev("ld_ffn"), 16)
            sp.dma_start(raw[:, LA, :], L1_ffn_lora_A.rearrange("e r d -> (e r) d")).then_inc(ev("ld_ffn"), 16)
            sp.dma_start(raw[:, WO:WO + FC, :], L1_ffn_wo.rearrange("d (c f) -> d c f", c=FC)).then_inc(ev("ld_ffn"), 16)
            for c in range(FC):
                sp.dma_start(raw[:, LB + c, :].rearrange("f (e r) -> f e r", e=E),
                             L1_ffn_lora_B[:, c * P:(c + 1) * P, :].rearrange("e f r -> f e r")).then_inc(ev("ld_ffn"), 16)
            sp.dma_start(bob, L1_ffn_bo.unsqueeze(0).to_broadcast([P, D])).then_inc(ev("ld_ffn"), 16)
            sp.dma_start(gbb, L1_ffn_gate_b.unsqueeze(0).to_broadcast([P, E])).then_inc(ev("ld_ffn"), 16)
            for k in range(4):
                sp.wait_ge(ev("y_ready"), k + 1)
                sp.dma_start(out[k // 2, (k % 2) * 512:(k % 2) * 512 + 512, :].rearrange("(t p) d -> p t d", p=P),
                             x[:, 4 * k:4 * k + 4, :]).then_inc(ev("stored"), 16)
            sp.wait_ge(ev("stored"), 64)
            sp.wait_ge(ev("slots_stored"), 16 * E)
            sp.wait_ge(ev("slots_zeroed"), 16)

        @block.gpsimd
        def _(pool):
            steps = [0]

            def link(ins):
                steps[0] += 1
                ins.then_inc(ev("pool_step"), 1)
                pool.wait_ge(ev("pool_step"), steps[0])

            link(pool.memset(ident[:, :], 0.0))
            pool.affine_select(out=ident[:, :], in_=ident[:, :], compare_op=ALU.not_equal, fill=1.0, base=0,
                               pattern=[[-1, P]], channel_multiplier=1).then_inc(ev("consts"), 1)
            link(pool.memset(before, 1.0))
            pool.affine_select(out=before, in_=before, compare_op=ALU.is_gt, fill=0.0, base=0,
                               pattern=[[1, P]], channel_multiplier=-1).then_inc(ev("consts"), 1)
            link(pool.memset(causal, 0.0))
            pool.affine_select(out=causal, in_=causal, compare_op=ALU.is_ge, fill=NEG, base=0,
                               pattern=[[-1, P]], channel_multiplier=1).then_inc(ev("consts"), 1)
            pool.memset(hot1b[:, 0, :], 0.0).then_inc(ev("consts"), 1)
            pool.memset(ones, 1.0).then_inc(ev("consts"), 1)
            pool.iota(iota8, [[1, E]], base=-E, channel_multiplier=0,
                      allow_small_or_imprecise_dtypes=True).then_inc(ev("consts"), 1)
            pool.iota(iota_n, [[P, NT]], base=E * CAP, channel_multiplier=1,
                      allow_small_or_imprecise_dtypes=True).then_inc(ev("consts"), 1)
            pool.iota(iota_c, [[CAP, E]], base=0, channel_multiplier=0,
                      allow_small_or_imprecise_dtypes=True).then_inc(ev("consts"), 1)
            pool.memset(zero_rows, 0.0).then_inc(ev("zeros"), 1)
            pool.wait_ge(ev("slots_zeroed"), 16)
            pool.wait_ge(ev("slot_numbers"), 1)
            for t in range(NT):
                pool.indirect_dma_start(slots_in, bass.IndirectOffsetOnAxis(ap=slot_s[:, t:t + 1], axis=0),
                                        h[:, t, :], None).then_inc(ev("scattered"), 16)
            pool.wait_ge(ev("slots_stored"), 16 * E)
            for t in range(NT):
                pool.indirect_dma_start(tmp1[:, t, :], None, slots_out,
                                        bass.IndirectOffsetOnAxis(ap=slot_g[:, t:t + 1], axis=0)).then_inc(ev("gathered"), 16)
            pool.wait_ge(ev("gathered"), 16 * NT)

        @block.scalar
        def _(act):
            act.wait_ge(ev("rows_turned"), 1)
            act.copy(cols[:, 0:NROWS], MI[:, 0:NROWS]).then_inc(ev("cols_ready"), 1)
            act.wait_ge(ev("cols_ready"), 1)
            act.activation(siluT, cols[:, C_C:C_C + 4], ACT.Exp, scale=-1.0).then_inc(ev("silu_exp"), 1)
            act.wait_ge(ev("w0_turned"), 1)
            act.copy(w0T.rearrange("p w d -> p (w d)"), SC[0][:, 0:384]).then_inc(ev("w0T_ready"), 1)
            for k in range(4):
                act.wait_ge(ev("vec_full"), k + 1)
                act.mul(vec_sb[:, k * 512:(k + 1) * 512], four[k][0:H, :], -1.0).then_inc(ev("vec_ready"), 1)

            def copy_mod(layer):
                for b in range(B):
                    act.wait_ge(ev("mod_full"), 2 * layer + b + 1)
                    if layer == 1:
                        act.wait_ge(ev("mod0_used"), 1)
                    act.copy(mod[:, b, :, :].rearrange("p m d -> p (m d)"),
                             SC[1 - b][:, 0:768]).then_inc(ev("mod_copied"), 1)

            def norm(n):
                for b in range(B):
                    act.wait_ge(ev("var_ready"), 2 * n + b + 1)
                    act.activation(st[:, 3, tiles(b)], st[:, 2, tiles(b)], ACT.Sqrt).then_inc(ev("root_ready"), 1)
                for b in range(B):
                    act.wait_ge(ev("h_turned"), 2 * n + b + 1)
                    act.copy(hT[:, b * S:(b + 1) * S], SC[b][:, :]).then_inc(ev("hT_ready"), 1)

            copy_mod(0)
            norm(0)
            n_qk = 0
            for f, (kind, b, half) in enumerate(fills0):
                if kind == "v":
                    continue
                act.wait_ge(ev("proj0_full"), f + 1)
                dst, col = (q0T, C_BQ) if kind == "q" else (k0T, C_BK)
                act.activation(dst[:, b * S + half * 512:b * S + half * 512 + 512], four[f % 4], ACT.Identity,
                               bias=cols[:, col:col + 1]).then_inc(ev("qk0_out"), 1)
                n_qk += 1
            for i in range(NT + 2):
                if i < NT:
                    w = (i % TB + 1) * P
                    act.wait_ge(ev("nmax0"), i + 1)
                    if i >= 2:
                        act.wait_ge(ev("pt0B_full"), i - 1)
                    act.activation(probs[:, i % 2, 0:w], SC[i % 2][:, 0:w], ACT.Exp, bias=nmax[:, i % 4:i % 4 + 1],
                                   scale=QK_SCALE, accum_out=rsum[:, i % 8:i % 8 + 1]).then_inc(ev("exp0"), 1)
                if i >= 2:
                    j = i - 2
                    m = min(j % TB + 1, 4)
                    act.wait_ge(ev("pt0A_full"), j + 1)
                    if j >= 4:
                        act.wait_ge(ev("pv0"), j - 3)
                    act.copy(tmp[:, (j % 4) * TB:(j % 4) * TB + m, :].rearrange("p k q -> p (k q)"),
                             PT[0][:, 0:m * P]).then_inc(ev("pt0A_out"), 1)
            norm(1)
            act.wait_ge(ev("logits_shifted"), 1)
            act.activation(rt[:, 1, :, :], rt[:, 0, :, :], ACT.Exp).then_inc(ev("router_exp"), 1)
            for k in range(0, 6, 2):
                act.wait_ge(ev("slots_turned"), k + 1)
                act.copy(slotT[:, k * 512:(k + 1) * 512], four[k % 4]).then_inc(ev("slotT_act"), 1)
            for e in range(E):
                for c in range(FC):
                    act.wait_ge(ev("hidden_full"), e * FC + c + 1)
                    if e >= 2:
                        act.wait_ge(ev("expert_full"), e - 1)
                    act.activation(gelu[:, e % 2, c, 0:CAP], four_sc[c][:, 0:CAP], ACT.Gelu,
                                   bias=cols[:, e * FC + c:e * FC + c + 1]).then_inc(ev("gelu_out"), 1)
            copy_mod(1)
            norm(2)
            for c in range(6):
                act_chunk(act, 0, c)
            pair_act(act, 0, first=True)
            with act.Fori(1, PAIRS - 1) as p:
                pair_act(act, p)
            pair_act(act, PAIRS - 1, last=True)
            for i in range(STEPS, STEPS + 5):
                act_step(act, PAIRS - 1, i)
            act.wait_ge(ev("ffn_turned"), 1)
            act.copy(wT[:, 0:8, :].rearrange("p w d -> p (w d)"), SC[0][:, :]).then_inc(ev("wT_ready"), 1)
            act.copy(wT[:, 8:13, :].rearrange("p w d -> p (w d)"), SC[1][:, 0:640]).then_inc(ev("wT_ready"), 1)
            norm(3)
            act.wait_ge(ev("logits_shifted"), 2)
            act.activation(rt[:, 1, :, :], rt[:, 0, :, :], ACT.Exp).then_inc(ev("router_exp"), 1)
            for k in range(4):
                act.wait_ge(ev("low_full"), k + 1)
                if k >= 1:
                    act.wait_ge(ev("masked"), 2 * k)
                act.copy(lowrank, MI[:, :]).then_inc(ev("low_ready"), 1)
                for j in range(2):
                    for c in range(FC):
                        n = k * 8 + j * FC + c
                        act.wait_ge(ev("inter_full"), n + 1)
                        if k >= 1 and j == 0 and c == 0:
                            act.wait_ge(ev("y_full"), k)
                        act.activation(act_r[:, j, c, :], four_sc[n % 4], ACT.Relu,
                                       bias=cols[:, C_BI + c:C_BI + c + 1]).then_inc(ev("relu_out"), 1)

        @block.vector
        def _(dve):
            steps = [0]

            def link(ins):
                steps[0] += 1
                ins.then_inc(ev("dve_step"), 1)
                dve.wait_ge(ev("dve_step"), steps[0])

            tt, ts, red = dve.tensor_tensor, dve.tensor_scalar, dve.tensor_reduce
            dve.wait_ge(ev("silu_exp"), 1)
            link(ts(siluT, siluT, 1.0, None, ALU.add))
            link(dve.reciprocal(siluT, siluT))
            tt(siluT, siluT, cols[:, C_C:C_C + 4], ALU.mult).then_inc(ev("silu_ready"), 1)

            def mod_finish(layer):
                for b in range(B):
                    dve.wait_ge(ev("mod_copied"), 2 * layer + b + 1)
                    for m in (1, 4):
                        link(ts(mod[:, b, m, :], mod[:, b, m, :], 1.0, None, ALU.add))
                    for m in (2, 5):
                        g, up, down, pos = mod[:, b, m, :], tmp2[:, 0, :], tmp2[:, 1, :], tmp2[:, 2, :]
                        link(ts(pos, g, 0.0, None, ALU.is_ge))
                        link(ts(up, g, 0.25, None, ALU.max))
                        link(ts(down, g, -0.25, None, ALU.min))
                        link(tt(up, up, down, ALU.subtract))
                        link(tt(up, up, pos, ALU.mult))
                        link(tt(g, up, down, ALU.add))

            def norm(n):
                m = 3 * (n % 2)
                for b in range(B):
                    if n == 0:
                        dve.wait_ge(ev("ld_x%d" % b), 16)
                    xb, hb, t = x[:, tiles(b), :], h[:, tiles(b), :], tmp1[:, tiles(b), :]
                    link(red(st[:, 0, tiles(b)], xb, AX.X, ALU.add))
                    link(ts(st[:, 0, tiles(b)], st[:, 0, tiles(b)], 1.0 / D, None, ALU.mult))
                    link(tt(hb, xb, bc_rows(st[:, 0, tiles(b)], D), ALU.subtract))
                    link(tt(t, hb, hb, ALU.mult))
                    link(red(st[:, 0, tiles(b)], t, AX.X, ALU.add))
                    ts(st[:, 2, tiles(b)], st[:, 0, tiles(b)], 1.0 / D, EPS, ALU.mult, ALU.add).then_inc(ev("var_ready"), 1)
                dve.wait_ge(ev("var_ready"), 2 * n + 2)
                for b in range(B):
                    dve.wait_ge(ev("root_ready"), 2 * n + b + 1)
                    root, var = st[:, 3, tiles(b)], st[:, 2, tiles(b)]
                    link(dve.reciprocal(st[:, 4, tiles(b)], root))
                    link(tt(st[:, 4, tiles(b)], st[:, 4, tiles(b)], var, ALU.mult))
                    link(tt(st[:, 4, tiles(b)], st[:, 4, tiles(b)], root, ALU.add))
                    link(ts(st[:, 4, tiles(b)], st[:, 4, tiles(b)], 0.5, None, ALU.mult))
                    link(dve.reciprocal(st[:, 5, tiles(b)], st[:, 4, tiles(b)]))
                    hb = h[:, tiles(b), :]
                    link(tt(hb, hb, bc_rows(st[:, 5, tiles(b)], D), ALU.mult))
                    link(tt(hb, hb, bc_tiles(mod[:, b, m + 1, :], TB), ALU.mult))
                    tt(hb, hb, bc_tiles(mod[:, b, m, :], TB), ALU.add).then_inc(ev("h_ready"), 1)

            mod_finish(0)
            norm(0)
            dve.wait_ge(ev("ld_bv"), 16)
            for f, (kind, b, half) in enumerate(fills0):
                if kind != "v":
                    continue
                dve.wait_ge(ev("proj0_full"), f + 1)
                t0 = b * TB + 4 * half
                tt(v0[:, t0:t0 + 4, :], four[f % 4].rearrange("p (t d) -> p t d", d=D), bc_tiles(bvb, 4),
                   ALU.add).then_inc(ev("v0_out"), 1)
            dve.wait_ge(ev("consts"), 8)
            for i in range(NT + 4):
                if i < NT:
                    w = (i % TB + 1) * P
                    dve.wait_ge(ev("scores0"), i + 1)
                    link(tt(SC[i % 2][:, w - P:w], SC[i % 2][:, w - P:w], causal, ALU.add))
                    link(red(st[:, 6, i:i + 1], SC[i % 2][:, 0:w], AX.X, ALU.max))
                    ts(nmax[:, i % 4:i % 4 + 1], st[:, 6, i:i + 1], -QK_SCALE, None, ALU.mult).then_inc(ev("nmax0"), 1)
                if 2 <= i < NT + 2:
                    j = i - 2
                    m = j % TB + 1 - 4
                    dve.wait_ge(ev("pt0B_full"), j + 1)
                    if m > 0:
                        if j >= 4:
                            dve.wait_ge(ev("pv0"), j - 3)
                        dve.tensor_copy(tmp[:, (j % 4) * TB + 4:(j % 4) * TB + 4 + m, :].rearrange("p k q -> p (k q)"),
                                        PT[1][:, 0:m * P]).then_inc(ev("pt0B_out"), 1)
                if i >= 4:
                    j = i - 4
                    dve.wait_ge(ev("pv0"), j + 1)
                    link(dve.reciprocal(rinv[:, j % 4:j % 4 + 1], rsum[:, j % 8:j % 8 + 1]))
                    link(dve.scalar_tensor_tensor(out=Rsb[:, 0, :], in0=CX0[j % 2],
                                                  scalar=rinv[:, j % 4:j % 4 + 1], in1=mod[:, j // TB, 2, :],
                                                  op0=ALU.mult, op1=ALU.mult))
                    ins = tt(x[:, j, :], x[:, j, :], Rsb[:, 0, :], ALU.add)
                    ins.then_inc(ev("att0_out"), 1)
                    dve.wait_ge(ev("att0_out"), j + 1)
            norm(1)

            def router_probs(n):
                lg = MI[:, 0:NT * E].rearrange("p (t e) -> p t e", e=E)
                dve.wait_ge(ev("logits_full"), n + 1)
                if n == 1:
                    dve.wait_ge(ev("ld_ffn"), 16 * 9)
                    link(tt(rt[:, 0, :, :], lg, bc_tiles(gbb, NT), ALU.add))
                else:
                    link(dve.tensor_copy(rt[:, 0, :, :], lg))
                link(red(st[:, 7, :], rt[:, 0, :, :], AX.X, ALU.max))
                tt(rt[:, 0, :, :], rt[:, 0, :, :], bc_rows(st[:, 7, :], E), ALU.subtract).then_inc(ev("logits_shifted"), 1)
                dve.wait_ge(ev("router_exp"), n + 1)
                link(red(st[:, 6, :], rt[:, 1, :, :], AX.X, ALU.add))
                link(dve.reciprocal(st[:, 6, :], st[:, 6, :]))
                link(tt(rt[:, 0, :, :], rt[:, 1, :, :], bc_rows(st[:, 6, :], E), ALU.mult))

            def first_max(best, hot):
                link(red(best, rt[:, 0, :, :], AX.X, ALU.max))
                link(tt(rt[:, 1, :, :], rt[:, 0, :, :], bc_rows(best, E), ALU.is_equal))
                link(tt(rt[:, 1, :, :], rt[:, 1, :, :], bc_tiles(iota8, NT), ALU.mult))
                link(red(st[:, 6, :], rt[:, 1, :, :], AX.X, ALU.min))
                link(tt(hot, bc_tiles(iota8, NT), bc_rows(st[:, 6, :], E), ALU.is_equal))

            router_probs(0)
            first_max(st[:, 7, :], rt[:, 2, :, :])
            dve.tensor_copy(hot1b[:, 1:, :], rt[:, 2, :, :]).then_inc(ev("hot_ready"), 1)
            link(tt(rt[:, 3, :, :], rt[:, 2, :, :], bc_tiles(iota_c, NT), ALU.mult))
            link(red(st[:, 5, :], rt[:, 3, :, :], AX.X, ALU.add))
            dve.wait_ge(ev("ranks_full"), 1)
            link(tt(rt[:, 3, :, :], rt[:, 2, :, :], MI[:, P:2 * P].rearrange("p (t e) -> p t e", e=E), ALU.mult))
            link(red(st[:, 4, :], rt[:, 3, :, :], AX.X, ALU.add))
            link(ts(st[:, 3, :], st[:, 4, :], float(CAP), None, ALU.is_lt))
            link(tt(st[:, 7, :], st[:, 7, :], st[:, 3, :], ALU.mult))
            link(tt(st[:, 6, :], st[:, 4, :], st[:, 5, :], ALU.add))
            link(tt(st[:, 6, :], st[:, 6, :], iota_n, ALU.subtract))
            link(tt(st[:, 6, :], st[:, 6, :], st[:, 3, :], ALU.mult))
            link(tt(slot_s, st[:, 6, :], iota_n, ALU.add))
            link(ts(st[:, 4, :], st[:, 4, :], float(CAP - 1), None, ALU.min))
            tt(slot_g, st[:, 4, :], st[:, 5, :], ALU.add).then_inc(ev("slot_numbers"), 1)
            for k in range(1, 6, 2):
                dve.wait_ge(ev("slots_turned"), k + 1)
                dve.tensor_copy(slotT[:, k * 512:(k + 1) * 512], four[k % 4]).then_inc(ev("slotT_dve"), 1)
            dve.wait_ge(ev("ld_b2"), 16)
            for e in range(E):
                dve.wait_ge(ev("expert_full"), e + 1)
                tt(slot_rows[:, e * CT:(e + 1) * CT, :], PT[e % 2][:, 0:CAP].rearrange("p (t d) -> p t d", d=D),
                   bc_tiles(b2b[:, e, :], CT), ALU.add).then_inc(ev("expert_out"), 1)
            dve.wait_ge(ev("gathered"), 16 * NT)
            for b in range(B):
                y = tmp1[:, tiles(b), :]
                link(tt(y, y, bc_rows(st[:, 7, tiles(b)], D), ALU.mult))
                link(tt(y, y, bc_tiles(mod[:, b, 5, :], TB), ALU.mult))
                link(tt(x[:, tiles(b), :], x[:, tiles(b), :], y, ALU.add))
            ts(st[:, 6, :], st[:, 7, :], 1.0, None, ALU.mult).then_inc(ev("mod0_used"), 1)
            dve.wait_ge(ev("mod0_used"), 1)
            mod_finish(1)
            norm(2)
            for c in range(6):
                dve_chunk(dve, 0, c)
            pair_dve(dve, 0, first=True)
            with dve.Fori(1, PAIRS - 1) as p:
                pair_dve(dve, p)
            pair_dve(dve, PAIRS - 1, last=True)
            for i in range(STEPS, STEPS + 6):
                dve_step(dve, PAIRS - 1, i)
            for k in range(4):
                dve.wait_ge(ev("wo_full"), k + 1)
                y = tmp1[:, 0:4, :]
                link(tt(y, four[k].rearrange("p (t d) -> p t d", d=D), bc_tiles(mod[:, k // 2, 2, :], 4), ALU.mult))
                link(tt(x[:, 4 * k:4 * k + 4, :], x[:, 4 * k:4 * k + 4, :], y, ALU.add))
            norm(3)
            router_probs(1)
            first_max(st[:, 7, :], rt[:, 2, :, :])
            link(dve.scalar_tensor_tensor(out=rt[:, 0, :, :], in0=rt[:, 2, :, :], scalar=-2.0, in1=rt[:, 0, :, :],
                                          op0=ALU.mult, op1=ALU.add))
            first_max(st[:, 5, :], rt[:, 3, :, :])
            ts(st[:, 4, :], st[:, 5, :], 1.0, None, ALU.mult).then_inc(ev("hot2_ready"), 1)
            dve.wait_ge(ev("hot2_ready"), 1)
            link(tt(st[:, 7, :], st[:, 7, :], st[:, 5, :], ALU.add))
            for k in range(4):
                for j in range(2):
                    dve.tensor_copy(hot_wide[:, j, :, :].rearrange("p t (e r) -> p t e r", e=E),
                                    rt[:, 2 + j, 4 * k:4 * k + 4, :].unsqueeze(3).to_broadcast([P, 4, E, R])).then_inc(ev("hot_wide"), 1)
                dve.wait_ge(ev("low_ready"), k + 1)
                for j in range(2):
                    dve.wait_ge(ev("mask_full"), 2 * k + j + 1)
                    if k >= 1:
                        dve.wait_ge(ev("inter_full"), 8 * k)
                    tt(masked[:, j, :], PT[j][:, :], lowrank, ALU.mult).then_inc(ev("masked"), 1)
                for c in range(FC):
                    dve.wait_ge(ev("relu_out"), 8 * k + FC + c + 1)
                    tt(act_r[:, 0, c, :], act_r[:, 0, c, :], act_r[:, 1, c, :], ALU.add).then_inc(ev("hidden_sum"), 1)
                dve.wait_ge(ev("y_full"), k + 1)
                y = h[:, 4 * k:4 * k + 4, :]
                link(dve.scalar_tensor_tensor(out=y, in0=bc_tiles(bob, 4), scalar=2.0,
                                              in1=CX[:, :].rearrange("p (t d) -> p t d", d=D), op0=ALU.mult, op1=ALU.add))
                link(tt(y, y, bc_rows(st[:, 7, 4 * k:4 * k + 4], D), ALU.mult))
                link(tt(y, y, bc_tiles(mod[:, k // 2, 5, :], 4), ALU.mult))
                tt(x[:, 4 * k:4 * k + 4, :], x[:, 4 * k:4 * k + 4, :], y, ALU.add).then_inc(ev("y_ready"), 1)

        @block.tensor
        def _(pe):
            mm = pe.matmul
            pe.wait_ge(ev("consts"), 8)
            pe.wait_ge(ev("ld_rows"), 16 * 8)
            pe.transpose(MI[:, 0:NROWS], rows[0:NROWS, :], ident[0:NROWS, 0:NROWS]).then_inc(ev("rows_turned"), 1)
            pe.wait_ge(ev("ld_w0"), 48)
            for n in range(3):
                ins = pe.transpose(SC[0][:, n * P:(n + 1) * P], w0raw[:, n, :], ident[:, :])
            ins.then_inc(ev("w0_turned"), 1)
            pe.wait_ge(ev("ld_rel"), 32)
            pe.wait_ge(ev("cols_ready"), 1)
            for k in range(4):
                mm(four[k][0:H, :], rel_sb, hot_sb[:, k * 512:(k + 1) * 512], start=True, stop=True).then_inc(ev("vec_full"), 1)

            def modulation(layer):
                for b in range(B):
                    lhs = siluT[:, 2 * layer + b:2 * layer + b + 1].to_broadcast([P, P])
                    mm(SC[1 - b][:, 0:512], lhs, wmod[layer][:, 0:512], start=True, stop=True)
                    mm(SC[1 - b][:, 512:768], lhs, wmod[layer][:, 512:768], start=True, stop=True).then_inc(ev("mod_full"), 1)

            pe.wait_ge(ev("silu_ready"), 1)
            pe.wait_ge(ev("ld_wmod"), 16)
            pe.wait_ge(ev("w0T_ready"), 1)
            modulation(0)

            def norm(n):
                for b in range(B):
                    pe.wait_ge(ev("h_ready"), 2 * n + b + 1)
                    for t in range(TB):
                        ins = pe.transpose(SC[b][:, t * P:(t + 1) * P], h[:, b * TB + t, :], ident[:, :])
                    ins.then_inc(ev("h_turned"), 1)

            pe.wait_ge(ev("mod_copied"), 2)
            norm(0)
            pe.wait_ge(ev("vec_ready"), 4)
            for f, (kind, b, half) in enumerate(fills0):
                if f >= 4:
                    name, n = out_of(f - 4)
                    pe.wait_ge(ev(name), n)
                pe.wait_ge(ev("hT_ready"), b + 1)
                at = b * S + half * 512
                if kind == "v":
                    for t in range(4):
                        ins = mm(four[f % 4][:, t * P:(t + 1) * P], hT[:, at + t * P:at + (t + 1) * P], w0T[:, 2, :],
                                 start=True, stop=True)
                else:
                    ins = mm(four[f % 4], w0T[:, "qk".index(kind), :], hT[:, at:at + 512], start=True, stop=True)
                ins.then_inc(ev("proj0_full"), 1)
            pe.wait_ge(ev("qk0_out"), 8)
            pe.wait_ge(ev("v0_out"), 4)
            for i in range(NT + 3):
                if i < NT:
                    b, w = i // TB, (i % TB + 1) * P
                    if i >= 2:
                        pe.wait_ge(ev("exp0"), i - 1)
                    for k in range(0, w, 512):
                        m = min(512, w - k)
                        ins = mm(SC[i % 2][:, k:k + m], q0T[:, i * P:(i + 1) * P], k0T[:, b * S + k:b * S + k + m],
                                 start=True, stop=True)
                    ins.then_inc(ev("scores0"), 1)
                if 2 <= i < NT + 2:
                    j = i - 2
                    pe.wait_ge(ev("exp0"), j + 1)
                    if j >= 1:
                        pe.wait_ge(ev("pt0A_out"), j)
                    nB = sum(1 for a in range(j) if a % TB >= 4)
                    if nB:
                        pe.wait_ge(ev("pt0B_out"), nB)
                    n = j % TB + 1
                    for t in range(n):
                        ins = pe.transpose(PT[t // 4][:, (t % 4) * P:(t % 4) * P + P], probs[:, j % 2, t * P:(t + 1) * P],
                                           ident[:, :])
                        if t == min(n, 4) - 1:
                            ins.then_inc(ev("pt0A_full"), 1)
                            if n <= 4:
                                pe.wait_ge(ev("pt0A_full"), j + 1)
                                pe.sem_inc(ev("pt0B_full"), 1)
                    if n > 4:
                        ins.then_inc(ev("pt0B_full"), 1)
                if i >= 3:
                    j = i - 3
                    pe.wait_ge(ev("pt0A_out"), j + 1)
                    nB = sum(1 for a in range(j + 1) if a % TB >= 4)
                    if nB:
                        pe.wait_ge(ev("pt0B_out"), nB)
                    if j >= 2:
                        pe.wait_ge(ev("att0_out"), j - 1)
                    n = j % TB + 1
                    for t in range(n):
                        ins = mm(CX0[j % 2], tmp[:, (j % 4) * TB + t, :],
                                 v0[:, j // TB * TB + t, :], start=(t == 0), stop=(t == n - 1))
                    ins.then_inc(ev("pv0"), 1)
            norm(1)

            def logits(n, col):
                pe.wait_ge(ev("hT_ready"), 2 * (2 * n + 1) + 2)
                for t in range(NT):
                    ins = mm(MI[:, t * E:(t + 1) * E], hT[:, t * P:(t + 1) * P], cols[:, col:col + E], start=True, stop=True)
                ins.then_inc(ev("logits_full"), 1)

            logits(0, C_RW)
            pe.wait_ge(ev("hot_ready"), 1)
            for t in range(NT):
                mm(MI[:, P + t * E:2 * P], ones, hot1b[:, t:t + 1, :].to_broadcast([P, NT - t, E]),
                   start=(t == 0), stop=False, skip_group_check=True)
            ins = mm(MI[:, P:2 * P], before, hot1b[:, 1:, :].rearrange("p t e -> p (t e)"), start=False, stop=True,
                     skip_group_check=True)
            ins.then_inc(ev("ranks_full"), 1)
            pe.wait_ge(ev("slots_loaded"), 16)
            pe.wait_ge(ev("slot_numbers"), 1)
            for k in range(6):
                if k >= 4:
                    pe.wait_ge(ev("slotT_act" if k % 2 == 0 else "slotT_dve"), (k - 4) // 2 + 1)
                for t in range(4):
                    ins = pe.transpose(four[k % 4][:, t * P:(t + 1) * P], slot_rows[:, 4 * k + t, :], ident[:, :])
                ins.then_inc(ev("slots_turned"), 1)
            pe.wait_ge(ev("slotT_act"), 3)
            pe.wait_ge(ev("slotT_dve"), 3)
            pe.wait_ge(ev("ld_w1"), 16)
            pe.wait_ge(ev("ld_w2"), 16)
            for e in range(E + 1):
                if e < E:
                    for c in range(FC):
                        if e >= 1:
                            pe.wait_ge(ev("gelu_out"), (e - 1) * FC + c + 1)
                        mm(four_sc[c][:, 0:CAP], w1[:, e, c * P:(c + 1) * P], slotT[:, e * CAP:(e + 1) * CAP],
                           start=True, stop=True).then_inc(ev("hidden_full"), 1)
                if e >= 1:
                    d = e - 1
                    pe.wait_ge(ev("gelu_out"), d * FC + FC)
                    if d >= 2:
                        pe.wait_ge(ev("expert_out"), d - 1)
                    for t in range(CT):
                        for c in range(FC):
                            ins = mm(PT[d % 2][:, t * P:(t + 1) * P], gelu[:, d % 2, c, t * P:(t + 1) * P], w2[:, d, c, :],
                                     start=(c == 0), stop=(c == FC - 1))
                    ins.then_inc(ev("expert_full"), 1)
            pe.wait_ge(ev("ld_wmod1"), 16)
            pe.wait_ge(ev("gelu_out"), E * FC)
            modulation(1)
            pe.wait_ge(ev("mod_copied"), 4)
            norm(2)
            pe.wait_ge(ev("hT_ready"), 6)
            for c in range(6):
                pe_chunk(pe, 0, c)
            pair_pe(pe, 0, first=True)
            with pe.Fori(1, PAIRS - 1) as p:
                pair_pe(pe, p)
            pair_pe(pe, PAIRS - 1, last=True)
            for i in range(STEPS, STEPS + 4):
                pe_step(pe, PAIRS - 1, i)
            pe.wait_ge(ev("ctx_out"), STEPS // 2 * PAIRS)
            pe.wait_ge(ev("ld_wo"), 16)
            for k in range(4):
                for t in range(4):
                    for a in range(PAIRS):
                        lhs = ctxT[:, a, (4 * k + t) * P:(4 * k + t + 1) * P]
                        ins = mm(four[k][:, t * P:(t + 1) * P], lhs, woall[:, a, :], start=(a == 0), stop=(a == PAIRS - 1))
                ins.then_inc(ev("wo_full"), 1)
            pe.wait_ge(ev("ld_ffn"), 16 * 9)
            for n in range(13):
                ins = pe.transpose(SC[n // 8][:, (n % 8) * P:(n % 8) * P + P], raw[:, n, :], ident[:, :])
            ins.then_inc(ev("ffn_turned"), 1)
            pe.wait_ge(ev("wT_ready"), 2)
            norm(3)
            logits(1, C_GW)
            pe.wait_ge(ev("logits_shifted"), 2)
            for k in range(4):
                hk = hT[:, k * 512:(k + 1) * 512]
                if k >= 1:
                    pe.wait_ge(ev("low_ready"), k)
                mm(MI[:, :], wT[:, LA, :], hk, start=True, stop=True).then_inc(ev("low_full"), 1)
                for j in range(2):
                    pe.wait_ge(ev("hot_wide"), 2 * k + j + 1)
                    if k >= 1:
                        pe.wait_ge(ev("masked"), 2 * (k - 1) + j + 1)
                    for t in range(4):
                        ins = pe.transpose(PT[j][:, t * P:(t + 1) * P], hot_wide[:, j, t, :], ident[:, :])
                    ins.then_inc(ev("mask_full"), 1)
                for j in range(2):
                    for c in range(FC):
                        n = k * 8 + j * FC + c
                        if n >= 4:
                            pe.wait_ge(ev("relu_out"), n - 3)
                        mm(four_sc[n % 4], wT[:, WI + c, :], hk, start=True, stop=False)
                        pe.wait_ge(ev("masked"), 2 * k + j + 1)
                        mm(four_sc[n % 4], wT[:, LB + c, :], masked[:, j, :], start=False, stop=True).then_inc(ev("inter_full"), 1)
                pe.wait_ge(ev("hidden_sum"), FC * (k + 1))
                if k >= 1:
                    pe.wait_ge(ev("y_ready"), k)
                for t in range(4):
                    for c in range(FC):
                        ins = mm(CX[:, t * P:(t + 1) * P], act_r[:, 0, c, t * P:(t + 1) * P], wT[:, WO + c, :],
                                 start=(c == 0), stop=(c == FC - 1))
                ins.then_inc(ev("y_full"), 1)

_INS = ['L0_attn_x', 'L0_attn_Wq', 'L0_attn_bq', 'L0_attn_Wk', 'L0_attn_bk', 'L0_attn_Wv', 'L0_attn_bv',
        'L0_ffn_router_w', 'L0_ffn_w1', 'L0_ffn_b1', 'L0_ffn_w2', 'L0_ffn_b2', 'L0_c', 'L0_wmod',
        'L1_attn_Wq', 'L1_attn_Wk', 'L1_attn_Wv', 'L1_attn_Wo', 'L1_attn_rel_emb',
        'L1_ffn_wi', 'L1_ffn_bi', 'L1_ffn_wo', 'L1_ffn_bo', 'L1_ffn_lora_A', 'L1_ffn_lora_B',
        'L1_ffn_gate_w', 'L1_ffn_gate_b', 'L1_c', 'L1_wmod']


def kernel(**inputs):
    import concourse.bacc as bacc
    from concourse.bass_utils import run_bass_kernel_spmd

    nc = bacc.Bacc("TRN2", target_bir_lowering=False, num_devices=1,
                   dynamic_dma_scratch_size=8192)
    arrays, args = {}, []
    for name in ["rel_hot"] + _INS:
        a = rel_one_hot() if name == "rel_hot" else np.ascontiguousarray(inputs[name])
        arrays["in_" + name] = a
        args.append(nc.dram_tensor("in_" + name, a.shape, mybir.dt.from_np(a.dtype), kind="ExternalInput").ap())
    args.append(nc.dram_tensor("out_0", (B, S, D), F32, kind="ExternalOutput").ap())
    build(nc, *args)
    r = run_bass_kernel_spmd(nc, [arrays], core_ids=[0])
    return r.results[0]["out_0"]
```

```python
from contextlib import ExitStack

import numpy as np

import concourse.bass as bass
from concourse import mybir

F32 = mybir.dt.float32
F32R = mybir.dt.float32r
BF16 = mybir.dt.bfloat16
U32 = mybir.dt.uint32
ALU = mybir.AluOpType
ACT = mybir.ActivationFunctionType
AX = mybir.AxisListType

P = 128
B, S, D = 2, 1024, 128
TB = S // P
NT = B * TB
E = 8
F = 512
FC = F // P
N = B * S
CAP = -(-3 * N // (2 * E))
CT = CAP // P
H, DK = 16, 64
PAIRS = H // 2
R = 16
BUCKETS = 32
EPS = 1e-5
QK_SCALE = float(D) ** -0.5
NEG = -3.0e38
VEC = 2048
STRIP = S + (TB - 1) * P
CK = 512
STEPS = 4 * TB
UNIT = 2 * TB
ROWS = 64


def rel_one_hot():
    hot = np.zeros((BUCKETS, VEC), np.float32)
    for col in range(VEC - 1):
        rel = col - (S - 1)
        n = abs(rel)
        if n < 8:
            bucket = n
        else:
            bucket = min(8 + (n * n // 64).bit_length() - 1, 15)
        hot[bucket + (16 if rel > 0 else 0), col] = 1.0
    return hot


def build(nc, rel_hot, L0_attn_x, L0_attn_Wq, L0_attn_bq, L0_attn_Wk, L0_attn_bk, L0_attn_Wv, L0_attn_bv,
          L0_ffn_router_w, L0_ffn_w1, L0_ffn_b1, L0_ffn_w2, L0_ffn_b2, L0_c, L0_wmod,
          L1_attn_Wq, L1_attn_Wk, L1_attn_Wv, L1_attn_Wo, L1_attn_rel_emb,
          L1_ffn_wi, L1_ffn_bi, L1_ffn_wo, L1_ffn_bo, L1_ffn_lora_A, L1_ffn_lora_B,
          L1_ffn_gate_w, L1_ffn_gate_b, L1_c, L1_wmod, out):
    with ExitStack() as ctx:
        ctx.enter_context(nc.allow_non_contiguous_dma(reason="small weight rearrangements"))

        def sb(name, shape, dt=F32):
            return ctx.enter_context(nc.sbuf_tensor(name, shape, dt))

        def ps(name, cols):
            return ctx.enter_context(nc.psum_tensor(name, [P, cols], F32))

        def sem(name):
            return ctx.enter_context(nc.semaphore(name))

        slots_in = nc.dram_tensor("slots_in", (E * CAP + N, D), F32, kind="Internal").ap()
        slots_out = nc.dram_tensor("slots_out", (E * CAP, D), F32, kind="Internal").ap()
        x_saved = nc.dram_tensor("x_saved", (N, D), F32, kind="Internal").ap().rearrange("(t p) d -> p t d", p=P)
        bias_vec = nc.dram_tensor("bias_vec", (H, VEC), F32, kind="Internal")

        with nc.sbuf_tensor("x", [P, NT, D], F32) as x:
            pass
        h_high = sb("h_high", [P, N], F32R)
        with nc.sbuf_tensor("arena", [P, PAIRS * N], F32) as arena:
            pass
        sb("arena_head", [P, (PAIRS - 1) * N])
        h_low = sb("h_low", [P, N], F32R)
        h_parts = (h_high, h_low)
        hT = sb("hT", [P, N])
        ident = sb("ident", [P, P])
        mod = sb("mod", [P, 2, B, 4, D])
        modc = sb("modc", [P, 2, 4, B])
        bst = sb("bst", [P, NT, 6])
        mv = sb("mv", [P, NT, 2])
        cols = sb("cols", [P, ROWS])
        probs = sb("probs", [P, 2, S])
        probsT = sb("probsT", [P, 2, 2, TB, P])
        QS = sb("QS", [P, 2, 2, S], F32R)
        KS = sb("KS", [P, 2, 2, 2, S], F32R)
        stage = sb("stage", [P, 4, CK], F32R)
        V1 = sb("V1", [P, 2, TB, P])
        wpair = sb("wpair", [P, 3, P])
        wsplit = sb("wsplit", [P, 2, 2, P], F32R)
        strips = sb("strips", [P, 2, 2, STRIP])
        Rsb = sb("Rsb", [P, 2, P])
        nmax = sb("nmax", [P, 4])
        rsum = sb("rsum", [P, 8])
        rinv = sb("rinv", [P, 4])
        rwide = sb("rwide", [P, 2, 2, DK])
        st = sb("st", [P, 8, NT])
        iota8 = st[:, 1, 0:E]

        ctxT = arena[:, :].rearrange("p (a n) -> p a n", a=PAIRS)

        def part(region, at, n):
            return region[:, at:at + n]

        w1 = part(arena, 0, E * F).rearrange("p (e f) -> p e f", e=E)
        w2 = part(arena, 4096, E * F).rearrange("p (e c d) -> p e c d", e=E, c=FC)
        slotT = part(arena, 8192, E * CAP)
        slot_rows = part(arena, 11264, E * CAP).rearrange("p (t d) -> p t d", t=E * CT)
        wmod = [part(arena, 14336, 768), part(arena, 15104, 768)]
        siluT = part(arena, 15872, 4)
        before = part(arena, 15876, 64).bitcast(BF16)
        ones = part(arena, 15940, 64).bitcast(BF16)
        hot1b = part(arena, 16004, 68).bitcast(BF16).rearrange("p (t e) -> p t e", e=E)
        slot_s = part(arena, 16072, NT).bitcast(U32)
        slot_g = part(arena, 16088, NT).bitcast(U32)
        iota_n = part(arena, 16104, NT)
        iota_c = part(arena, 16120, E)
        flat = strips[:, :, :, :].rearrange("p a h n -> p (a h n)")
        q0T, k0T = part(flat, 0, N), part(flat, N, N)
        v0 = part(flat, 2 * N, N).rearrange("p (t d) -> p t d", t=NT)
        w0raw = part(flat, 3 * N, 384).rearrange("p (w d) -> p w d", w=3)
        w0T = part(flat, 3 * N + 384, 384).rearrange("p (w d) -> p w d", w=3)
        bvb = part(flat, 3 * N + 768, D)
        raw = part(flat, 0, 13 * P).rearrange("p (w d) -> p w d", w=13)
        wT = part(flat, 13 * P, 13 * P).rearrange("p (w d) -> p w d", w=13)
        bob = part(flat, 26 * P, D)
        gbb = part(flat, 27 * P, E)
        woall = part(flat, 28 * P, PAIRS * D).rearrange("p (a d) -> p a d", a=PAIRS)
        lowrank = part(flat, 36 * P, 4 * P)
        masked = part(flat, 40 * P, 8 * P).rearrange("p (j n) -> p j n", j=2)
        hot_wide = part(flat, 0, 8 * P).rearrange("p (j t d) -> p j t d", j=2, t=4)
        h = probs[:, :, :].rearrange("p a (t d) -> p (a t) d", d=D)
        tmp = probsT[:, :, :, :, :].rearrange("p a h k q -> p (a h k) q")
        tmp1, tmp2 = tmp[:, 0:NT, :], tmp[:, NT:2 * NT, :]
        gates = mod[:, :, :, 0:4:3, :].rearrange("p l b m d -> p (l b) m d")
        g_up, g_down, g_pos = [tmp[:, 8 * k:8 * k + 8, :].rearrange("p (a m) d -> p a m d", m=2) for k in range(3)]
        gelu = tmp[:, 0:24, :].rearrange("p (a c t) q -> p a c (t q)", a=2, c=FC)
        act_r = tmp.rearrange("p (a c t) q -> p a c (t q)", a=2, c=FC)
        stage1 = tmp2.rearrange("p (w t) d -> p w (t d)", w=4).bitcast(F32R)
        b2b = V1[:, 0, :, :]
        rt = V1[:, 1, 1:7, :].rearrange("p a (t e) -> p a t e", e=E)
        causal = V1[:, 1, 7, :]
        rows = V1[0:ROWS, 1, 0, :]
        vec_sb = arena[0:H, 8192:8192 + VEC]
        hot_sb = arena[32:32 + BUCKETS, 8192:8192 + VEC]
        rel_sb = arena[32:32 + BUCKETS, 8192 + VEC:8192 + VEC + H]
        zero_rows = part(arena, 11264, E * CAP)

        SC = [ps("SC0", 2 * 512), ps("SC1", 2 * 512)]
        PT = [ps("PTA", 512), ps("PTB", 512)]
        CX = ps("CX", 512)
        MI = ps("MI", 512)
        CX0 = [CX[:, 0:P], MI[:, 0:P]]
        four = [PT[0][:, :], PT[1][:, :], CX[:, :], MI[:, :]]
        four_sc = [SC[0][:, 0:512], SC[0][:, 512:1024], SC[1][:, 0:512], SC[1][:, 512:1024]]

        sems = {}

        def ev(name):
            if name not in sems:
                sems[name] = ctx.enter_context(nc.semaphore("s_" + name))
            return sems[name]

        C_B1, C_BQ, C_BK, C_BI, C_C, C_RW, C_GW, NROWS = 0, 32, 33, 34, 38, 42, 50, 58
        WI, LA, WO, LB = 0, 4, 5, 9

        def bc_rows(ap, n):
            return ap.unsqueeze(2).to_broadcast([ap.shape[0], ap.shape[1], n])

        def bc_tiles(ap, n):
            return ap.unsqueeze(1).to_broadcast([ap.shape[0], n, ap.shape[1]])

        def tiles(b):
            return slice(b * TB, (b + 1) * TB)

        fills0 = [(kind, b, half) for b in range(B) for kind in "qkv" for half in range(2)]

        def out_of(f):
            mine = [g for g in range(f + 1) if (fills0[g][0] == "v") == (fills0[f][0] == "v")]
            return ("v0_out" if fills0[f][0] == "v" else "qk0_out"), len(mine)

        def load_strips(sp, copy, p):
            sp.dma_start(strips[:, copy, :, :],
                         bass.AP(bias_vec, p * (2 * VEC), [[1, P], [VEC, 2], [1, STRIP]])).then_inc(ev("strips%d" % copy), 16)

        def load_weights(sp, p):
            for n, w in enumerate((L1_attn_Wq, L1_attn_Wk, L1_attn_Wv)):
                sp.dma_start(wpair[:, n, :], w[:, bass.ts(p, P)]).then_inc(ev("ld_pair"), 16)

        def stack_half(sp, u, half):
            b, n = (u % 2, u) if isinstance(u, int) else (u[1], 2 * u[0] + u[1])
            for k in range(2):
                sp.wait_ge(ev("low_out"), 4 * n + 2 * half + k + 1)
                at = slice(half * 512, half * 512 + 512)
                for hd in range(2):
                    mine = slice(hd * DK, hd * DK + DK)
                    for side in range(2):
                        rows_ = slice(side * DK, side * DK + DK)
                        if k == 0:
                            sp.dma_start(QS[rows_, b, hd, at].bitcast(F32),
                                         stage_of(u, half)[mine, side, :].bitcast(F32)).then_inc(ev("stacked_q"), 16)
                        else:
                            sp.dma_start(KS[rows_, b, hd, :, at].bitcast(F32),
                                         stage_of(u, half)[mine, 2:4, :].bitcast(F32)).then_inc(ev("stacked_k"), 16)

        def pair_dma(sp, p, last=False):
            sp.wait_ge(ev("scores"), STEPS * p)
            for half in range(2):
                stack_half(sp, (p, 1), half)
            if last:
                return
            sp.wait_ge(ev("proj_full"), 12 * p + 12)
            load_weights(sp, p + 1)
            sp.wait_ge(ev("nmax_done"), STEPS * p + UNIT)
            load_strips(sp, 0, p + 1)
            for half in range(2):
                stack_half(sp, (p + 1, 0), half)
            sp.wait_ge(ev("nmax_done"), STEPS * p + STEPS)
            load_strips(sp, 1, p + 1)

        chunks = [("q", 0), ("k", 0), ("q", 1), ("k", 1), ("v", 0), ("v", 1)]

        def chunk_bank(u, c):
            return four[c % 4] if isinstance(u, int) else MI[:, :]

        def stage_of(u, q):
            return stage1 if isinstance(u, int) and q == 1 else stage[:, :, :]

        def has_chunk(i, last):
            return i < STEPS and i % 2 == 0 and i % UNIT < 12 and not (last and i >= UNIT)

        def act_chunk(act, u, c):
            b, n = (u % 2, u) if isinstance(u, int) else (u[1], 2 * u[0] + u[1])
            kind, q = chunks[c]
            act.wait_ge(ev("proj_full"), 6 * n + c + 1)
            if kind == "v":
                act.copy(V1[:, b, 4 * q:4 * q + 4, :].rearrange("p t d -> p (t d)"), chunk_bank(u, c)).then_inc(ev("high_out"), 1)
                return
            k = 0 if kind == "q" else 2
            if not isinstance(u, int):
                act.wait_ge(ev("stacked_" + kind), 64 * (2 * n + q))
            act.mul(stage_of(u, q)[:, k, :], chunk_bank(u, c), -1.0 if kind == "q" else 1.0).then_inc(ev("high_out"), 1)

        def act_step(act, p, i, first=False, last=False):
            n = STEPS * p + i
            G = STEPS // 2
            if i % 2 == 0 and not (first and i < 4) and i < STEPS + 4:
                g = i // 2 - 2
                act.wait_ge(ev("r_full"), G * p + g + 1)
                if not (first and g < 2):
                    act.wait_ge(ev("ctx_out"), G * p + g - 1)
                act.copy(Rsb[:, g % 2, :], MI[:, 0:P]).then_inc(ev("r_out"), 1)
            if not (first and i < 2) and i < STEPS + 2:
                j = (i - 2) % STEPS
                act.wait_ge(ev("ptA_full"), n - 1)
                if not (first and i < 6):
                    act.wait_ge(ev("pv_done"), G * p + (i - 2) // 2 - 1)
                act.copy(probsT[:, (j // 2) % 2, j % 2, 0:4, :].rearrange("p k q -> p (k q)"),
                         PT[0][:, :]).then_inc(ev("ptA_out"), 1)
            if i < STEPS:
                act.wait_ge(ev("nmax_done"), n + 1)
                if not (first and i < 2):
                    act.wait_ge(ev("ptB_full"), n - 1)
                act.activation(probs[:, i % 2, :], SC[i % 2][:, :], ACT.Exp, bias=nmax[:, i % 4:i % 4 + 1],
                               scale=-1.0, accum_out=rsum[:, i % 4:i % 4 + 1]).then_inc(ev("exp_done"), 1)
            if has_chunk(i, last):
                act_chunk(act, (p + i // UNIT, (i // UNIT + 1) % 2), i % UNIT // 2)

        def pair_act(act, p, first=False, last=False):
            for i in range(STEPS):
                act_step(act, p, i, first, last)

        def dve_chunk(dve, u, c):
            n = u if isinstance(u, int) else 2 * u[0] + u[1]
            kind, q = chunks[c]
            if kind == "v":
                return
            k = 0 if kind == "q" else 2
            dve.wait_ge(ev("high_out"), 6 * n + c + 1)
            dve.scalar_tensor_tensor(out=stage_of(u, q)[:, k + 1, :], in0=chunk_bank(u, c), scalar=-1.0 if kind == "q" else 1.0,
                                     in1=stage_of(u, q)[:, k, :].bitcast(F32), op0=ALU.mult, op1=ALU.subtract).then_inc(ev("low_out"), 1)

        def dve_step(dve, p, i, first=False, last=False):
            n = STEPS * p + i
            if i % 2 == 0 and not (first and i < 6):
                g = i // 2 - 3
                dve.wait_ge(ev("r_out"), STEPS // 2 * p + g + 1)
                dve.wait_ge(ev("pv_done"), STEPS // 2 * p + g + 1)
                gg = g % (STEPS // 2)
                pair = p if g >= 0 else p - 1
                dve.tensor_tensor(arena[:, bass.ds(pair * N + gg * P, P)],
                                  bass.AP(CX, P - 1, [[512, P], [-1, P]]),
                                  bass.AP(Rsb, (g % 2) * P + P - 1, [[2 * P, P], [-1, P]]), ALU.mult).then_inc(ev("ctx_out"), 1)
            if i < STEPS:
                b, qt, hd = i // UNIT, (i % UNIT) // 2, i % 2
                dve.wait_ge(ev("scores"), n + 1)
                if i % UNIT == 0:
                    dve.wait_ge(ev("strips%d" % b), 16 * (p + 1) if isinstance(p, int) else p * 16 + 16)
                at = (TB - 1 - qt) * P
                dve.sem_inc(ev("minimum_started"), 1)
                dve.tensor_tensor_reduce(SC[hd][:, :], SC[hd][:, :], strips[:, b, hd, at:at + S], 1.0, 3.4e38,
                                         ALU.add, ALU.min, nmax[:, i % 4:i % 4 + 1]).then_inc(ev("nmax_done"), 1)
            if not (first and i < 2) and i < STEPS + 2:
                j = (i - 2) % STEPS
                dve.wait_ge(ev("ptB_full"), n - 1)
                if not (first and i < 6):
                    dve.wait_ge(ev("pv_done"), STEPS // 2 * p + (i - 2) // 2 - 1)
                dve.tensor_copy(probsT[:, (j // 2) % 2, j % 2, 4:8, :].rearrange("p k q -> p (k q)"),
                                PT[1][:, :]).then_inc(ev("ptB_out"), 1)
            if has_chunk(i, last):
                dve_chunk(dve, (p + i // UNIT, (i // UNIT + 1) % 2), i % UNIT // 2)
            if i % 2 == 0 and not (first and i < 2) and i < STEPS + 2:
                j = (i - 2) % 4
                dve.wait_ge(ev("exp_done"), n)
                if not (first and i < 6):
                    dve.wait_ge(ev("r_full"), STEPS // 2 * p + i // 2 - 2)
                dve.reciprocal(rinv[:, j:j + 2], rsum[:, j:j + 2]).then_inc(ev("rinv_small"), 1)
                dve.wait_ge(ev("rinv_small"), STEPS // 2 * p + i // 2)
                dve.tensor_copy(rwide[:, j // 2, :, :], rinv[:, j:j + 2].unsqueeze(2).to_broadcast([P, 2, DK])).then_inc(ev("rinv_done"), 1)

        def pair_dve(dve, p, first=False, last=False):
            for i in range(STEPS):
                dve_step(dve, p, i, first, last)

        def pe_chunk(pe, u, c):
            b, n = (u % 2, u) if isinstance(u, int) else (u[1], 2 * u[0] + u[1])
            kind, q = chunks[c]
            if c == 0 and b == 0:
                pe.wait_ge(ev("w_split"), (u[0] if not isinstance(u, int) else 0) + 1)
            bank = chunk_bank(u, c)
            if isinstance(u, int):
                if c >= 4:
                    pe.wait_ge(ev("low_out"), c - 3)
            elif c >= 1 and chunks[c - 1][0] != "v":
                pe.wait_ge(ev("low_out"), 4 * n + c)
            else:
                pe.wait_ge(ev("high_out"), 6 * n + c)
            at = b * S + q * CK
            if kind == "v":
                for t in range(4):
                    ins = pe.matmul(bank[:, t * P:(t + 1) * P], hT[:, at + t * P:at + (t + 1) * P], wpair[:, 2, :],
                                    start=True, stop=True)
            else:
                for n, (hp, wp) in enumerate(((0, 0), (1, 0), (0, 1))):
                    rhs = h_parts[hp][:, at:at + CK]
                    if kind == "q":
                        rhs = bass.AP(h_parts[hp], at + P - 1, [[N, P], [P, CK // P], [-1, P]])
                    ins = pe.matmul(bank, wsplit[:, wp, "qk".index(kind), :], rhs, start=(n == 0), stop=(n == 2))
            ins.then_inc(ev("proj_full"), 1)

        def pe_step(pe, p, i, first=False, last=False):
            n = STEPS * p + i
            G = STEPS // 2
            if i < STEPS:
                b, qt, hd = i // UNIT, (i % UNIT) // 2, i % 2
                if i % UNIT == 0:
                    pe.wait_ge(ev("stacked_q"), p * 256 + 128 * (b + 1))
                    pe.wait_ge(ev("stacked_k"), p * 256 + 128 * (b + 1))
                if not (first and i < 2):
                    pe.wait_ge(ev("exp_done"), n - 1)
                lhs = QS[:, b, hd, qt * P:(qt + 1) * P]
                for k in range(2):
                    for part_ in range(2):
                        ins = pe.matmul(SC[hd][:, k * 512:(k + 1) * 512], lhs, KS[:, b, hd, part_, k * 512:(k + 1) * 512],
                                        start=(part_ == 0), stop=(part_ == 1))
                ins.then_inc(ev("scores"), 1)
            if not (first and i < 2) and i < STEPS + 2:
                j = (i - 2) % STEPS
                pe.wait_ge(ev("exp_done"), n - 1)
                for half in range(2):
                    if not (first and i < 3):
                        pe.wait_ge(ev("ptA_out" if half == 0 else "ptB_out"), n - 2)
                    for t in range(4):
                        ins = pe.transpose(PT[half][:, t * P:(t + 1) * P],
                                           probs[:, j % 2, (4 * half + t) * P:(4 * half + t + 1) * P], ident[:, :])
                    ins.then_inc(ev("ptA_full" if half == 0 else "ptB_full"), 1)
            if has_chunk(i, last):
                if not (first and i < 4):
                    pe.wait_ge(ev("r_out"), G * p + i // 2 - 1)
                pe_chunk(pe, (p + i // UNIT, (i // UNIT + 1) % 2), i % UNIT // 2)
            if not (first and i < 4):
                g, half = i // 2 - 2, i % 2
                gg = g % G
                vb = gg // TB
                pe.wait_ge(ev("ptA_out" if half == 0 else "ptB_out"), STEPS * p + 2 * g + 2)
                if half == 0 and not (first and g < 1):
                    pe.wait_ge(ev("ctx_out"), G * p + g)
                for t in range(4 * half, 4 * half + 4):
                    for hd in range(2):
                        ins = pe.matmul(CX[hd * DK:(hd + 1) * DK, 0:P],
                                        V1[:, vb, t, hd * DK:(hd + 1) * DK], probsT[:, gg % 2, hd, t, :],
                                        start=(t == 0), stop=(t == TB - 1))
                if half == 1:
                    ins.then_inc(ev("pv_done"), 1)
            if i % 2 == 1 and not (first and i < 3) and i < STEPS + 3:
                g = (i - 3) // 2
                pe.wait_ge(ev("rinv_done"), G * p + g + 1)
                if has_chunk((i - 1) % STEPS if i < STEPS else STEPS, last):
                    c, n6 = (i % UNIT) // 2, 2 * p + i // UNIT + 1
                    if c < 4:
                        pe.wait_ge(ev("low_out"), 4 * n6 + c + 1)
                    else:
                        pe.wait_ge(ev("high_out"), 6 * n6 + c + 1)
                if not (first and g < 1):
                    pe.wait_ge(ev("r_out"), G * p + g)
                pe.transpose(MI[:, 0:P], rwide[:, g % 2, :, :].rearrange("p h d -> p (h d)"),
                             ident[:, :]).then_inc(ev("r_full"), 1)

        def pair_pe(pe, p, first=False, last=False):
            for i in range(STEPS):
                pe_step(pe, p, i, first, last)


        block = ctx.enter_context(nc.Block())

        @block.sync
        def _(sp):
            sp.dma_start(rows[C_B1:C_B1 + 32, :], L0_ffn_b1.rearrange("e (c f) -> (e c) f", c=FC)).then_inc(ev("ld_rows"), 16)
            sp.dma_start(rows[C_BQ:C_BQ + 1, :], L0_attn_bq.unsqueeze(0)).then_inc(ev("ld_rows"), 16)
            sp.dma_start(rows[C_BK:C_BK + 1, :], L0_attn_bk.unsqueeze(0)).then_inc(ev("ld_rows"), 16)
            sp.dma_start(rows[C_BI:C_BI + FC, :], L1_ffn_bi.rearrange("(c f) -> c f", c=FC)).then_inc(ev("ld_rows"), 16)
            sp.dma_start(rows[C_C:C_C + 2, :], L0_c).then_inc(ev("ld_rows"), 16)
            sp.dma_start(rows[C_C + 2:C_C + 4, :], L1_c).then_inc(ev("ld_rows"), 16)
            sp.dma_start(rows[C_RW:C_RW + E, :], L0_ffn_router_w).then_inc(ev("ld_rows"), 16)
            sp.dma_start(rows[C_GW:C_GW + E, :], L1_ffn_gate_w).then_inc(ev("ld_rows"), 16)
            for b in range(B):
                sp.dma_start(x[:, tiles(b), :], L0_attn_x[b].rearrange("(t p) d -> p t d", p=P)).then_inc(ev("ld_x%d" % b), 16)
            sp.dma_start(wmod[0], L0_wmod).then_inc(ev("ld_wmod"), 16)
            for n, w in enumerate((L0_attn_Wq, L0_attn_Wk, L0_attn_Wv)):
                sp.dma_start(w0raw[:, n, :], w).then_inc(ev("ld_w0"), 16)
            sp.dma_start(bvb, L0_attn_bv.unsqueeze(0).to_broadcast([P, D])).then_inc(ev("ld_bv"), 16)
            sp.dma_start(hot_sb, rel_hot).then_inc(ev("ld_rel"), 16)
            sp.dma_start(rel_sb, L1_attn_rel_emb).then_inc(ev("ld_rel"), 16)
            sp.dma_start(wmod[1], L1_wmod).then_inc(ev("ld_wmod1"), 16)
            sp.dma_start(w1, L0_ffn_w1.rearrange("e d f -> d e f")).then_inc(ev("ld_w1"), 16)
            sp.dma_start(w2, L0_ffn_w2.rearrange("e (c f) d -> f e c d", c=FC)).then_inc(ev("ld_w2"), 16)
            sp.dma_start(b2b, L0_ffn_b2.unsqueeze(0).to_broadcast([P, E, D])).then_inc(ev("ld_b2"), 16)
            sp.wait_ge(ev("zeros"), 1)
            sp.dma_start(slots_in[0:E * CAP, :].rearrange("(p r) d -> p (r d)", p=P), zero_rows).then_inc(ev("slots_zeroed"), 16)
            sp.wait_ge(ev("vec_ready"), 4)
            sp.dma_start(bias_vec.ap(), vec_sb).then_inc(ev("vec_stored"), 16)
            sp.wait_ge(ev("vec_stored"), 16)
            load_weights(sp, 0)
            sp.wait_ge(ev("pv0"), NT)
            sp.wait_ge(ev("scores0"), NT)
            load_strips(sp, 0, 0)
            load_strips(sp, 1, 0)
            sp.wait_ge(ev("scattered"), 16 * NT)
            sp.dma_start(slot_rows, slots_in[0:E * CAP, :].rearrange("(t p) d -> p t d", p=P)).then_inc(ev("slots_loaded"), 16)
            for e in range(E):
                sp.wait_ge(ev("expert_out"), e + 1)
                sp.dma_start(slots_out[e * CAP:(e + 1) * CAP, :].rearrange("(t p) d -> p t d", p=P),
                             slot_rows[:, e * CT:(e + 1) * CT, :]).then_inc(ev("slots_stored"), 16)
            for b in range(B):
                sp.wait_ge(ev("x_quarter"), 2 * b + 2)
                sp.dma_start(x_saved[:, tiles(b), :], x[:, tiles(b), :]).then_inc(ev("x_saved%d" % b), 16)
            for half in range(2):
                stack_half(sp, 0, half)
            pair_dma(sp, 0)
            with sp.Fori(1, PAIRS - 1) as p:
                pair_dma(sp, p)
            pair_dma(sp, PAIRS - 1, last=True)
            sp.wait_ge(ev("proj_full"), 12 * PAIRS)
            sp.dma_start(x[:, :, :], x_saved).then_inc(ev("x_back"), 16)
            sp.wait_ge(ev("nmax_done"), STEPS * PAIRS)
            sp.dma_start(woall, L1_attn_Wo.rearrange("(a p) d -> p a d", p=P)).then_inc(ev("ld_wo"), 16)
            sp.dma_start(raw[:, WI:WI + FC, :], L1_ffn_wi.rearrange("(c p) d -> p c d", p=P)).then_inc(ev("ld_ffn"), 16)
            sp.dma_start(raw[:, LA, :], L1_ffn_lora_A.rearrange("e r d -> (e r) d")).then_inc(ev("ld_ffn"), 16)
            sp.dma_start(raw[:, WO:WO + FC, :], L1_ffn_wo.rearrange("d (c f) -> d c f", c=FC)).then_inc(ev("ld_ffn"), 16)
            for c in range(FC):
                sp.dma_start(raw[:, LB + c, :].rearrange("f (e r) -> f e r", e=E),
                             L1_ffn_lora_B[:, c * P:(c + 1) * P, :].rearrange("e f r -> f e r")).then_inc(ev("ld_ffn"), 16)
            sp.dma_start(bob, L1_ffn_bo.unsqueeze(0).to_broadcast([P, D])).then_inc(ev("ld_ffn"), 16)
            sp.dma_start(gbb, L1_ffn_gate_b.unsqueeze(0).to_broadcast([P, E])).then_inc(ev("ld_ffn"), 16)
            for k in range(4):
                sp.wait_ge(ev("y_ready"), k + 1)
                sp.dma_start(out[k // 2, (k % 2) * 512:(k % 2) * 512 + 512, :].rearrange("(t p) d -> p t d", p=P),
                             x[:, 4 * k:4 * k + 4, :]).then_inc(ev("stored"), 16)
            sp.wait_ge(ev("stored"), 64)
            sp.wait_ge(ev("slots_stored"), 16 * E)
            sp.wait_ge(ev("slots_zeroed"), 16)

        @block.gpsimd
        def _(pool):
            steps = [0]

            def link(ins):
                steps[0] += 1
                ins.then_inc(ev("pool_step"), 1)
                pool.wait_ge(ev("pool_step"), steps[0])

            link(pool.memset(ident[:, :], 0.0))
            pool.affine_select(out=ident[:, :], in_=ident[:, :], compare_op=ALU.not_equal, fill=1.0, base=0,
                               pattern=[[-1, P]], channel_multiplier=1).then_inc(ev("consts"), 1)
            link(pool.memset(before, 1.0))
            pool.affine_select(out=before, in_=before, compare_op=ALU.is_gt, fill=0.0, base=0,
                               pattern=[[1, P]], channel_multiplier=-1).then_inc(ev("consts"), 1)
            link(pool.memset(causal, 0.0))
            pool.affine_select(out=causal, in_=causal, compare_op=ALU.is_ge, fill=NEG, base=0,
                               pattern=[[-1, P]], channel_multiplier=1).then_inc(ev("consts"), 1)
            pool.memset(hot1b[:, 0, :], 0.0).then_inc(ev("consts"), 1)
            pool.memset(ones, 1.0).then_inc(ev("consts"), 1)
            pool.iota(iota8, [[1, E]], base=-E, channel_multiplier=0,
                      allow_small_or_imprecise_dtypes=True).then_inc(ev("consts"), 1)
            pool.iota(iota_n, [[P, NT]], base=E * CAP, channel_multiplier=1,
                      allow_small_or_imprecise_dtypes=True).then_inc(ev("consts"), 1)
            pool.iota(iota_c, [[CAP, E]], base=0, channel_multiplier=0,
                      allow_small_or_imprecise_dtypes=True).then_inc(ev("consts"), 1)
            pool.memset(zero_rows, 0.0).then_inc(ev("zeros"), 1)
            for b in range(B):
                pool.wait_ge(ev("h_ready"), 4 + 2 * b + 2)
                link(pool.tensor_tensor(tmp2[:, tiles(b), :], h[:, tiles(b), :], bc_tiles(mod[:, 0, b, 2, :], TB), ALU.mult))
                link(pool.tensor_tensor(tmp2[:, tiles(b), :], tmp2[:, tiles(b), :], bc_tiles(mod[:, 0, b, 1, :], TB), ALU.add))
            pool.wait_ge(ev("slots_zeroed"), 16)
            pool.wait_ge(ev("slot_numbers"), 1)
            for t in range(NT):
                pool.indirect_dma_start(slots_in, bass.IndirectOffsetOnAxis(ap=slot_s[:, t:t + 1], axis=0),
                                        tmp2[:, t, :], None).then_inc(ev("scattered"), 16)
            pool.wait_ge(ev("ld_pair"), 48)
            pool.tensor_copy(wsplit[:, 0, :, :], wpair[:, 0:2, :]).then_inc(ev("w_high"), 1)
            pool.wait_ge(ev("w_high"), 1)
            pool.tensor_tensor(wsplit[:, 1, :, :], wpair[:, 0:2, :], wsplit[:, 0, :, :].bitcast(F32),
                               ALU.subtract).then_inc(ev("w_split"), 1)
            pool.wait_ge(ev("slots_stored"), 16 * E)
            for t in range(NT):
                pool.indirect_dma_start(tmp1[:, t, :], None, slots_out,
                                        bass.IndirectOffsetOnAxis(ap=slot_g[:, t:t + 1], axis=0)).then_inc(ev("gathered%d" % (t // 4)), 16)
            for k in range(4):
                pool.wait_ge(ev("h_high"), k + 1)
                pool.tensor_tensor(h_low[:, k * 512:(k + 1) * 512], hT[:, k * 512:(k + 1) * 512], h_high[:, k * 512:(k + 1) * 512].bitcast(F32),
                                   ALU.subtract).then_inc(ev("h_split"), 1)
            with pool.Fori(1, PAIRS) as p:
                pool.wait_ge(ev("ld_pair"), 48 * p + 48)
                pool.wait_ge(ev("proj_full"), 12 * p)
                pool.sem_inc(ev("split_started"), 1)
                pool.tensor_copy(wsplit[:, 0, :, :], wpair[:, 0:2, :]).then_inc(ev("w_high"), 1)
                pool.wait_ge(ev("w_high"), p + 1)
                pool.sem_inc(ev("split_started"), 1)
                pool.tensor_tensor(wsplit[:, 1, :, :], wpair[:, 0:2, :], wsplit[:, 0, :, :].bitcast(F32),
                                   ALU.subtract).then_inc(ev("w_split"), 1)

        @block.scalar
        def _(act):
            act.wait_ge(ev("rows_turned"), 1)
            act.copy(cols[:, 0:NROWS], MI[:, 0:NROWS]).then_inc(ev("cols_ready"), 1)
            act.wait_ge(ev("cols_ready"), 1)
            act.activation(siluT, cols[:, C_C:C_C + 4], ACT.Exp, scale=-1.0).then_inc(ev("silu_exp"), 1)
            act.wait_ge(ev("w0_turned"), 1)
            act.copy(w0T.rearrange("p w d -> p (w d)"), SC[0][:, 0:384]).then_inc(ev("w0T_ready"), 1)
            for k in range(4):
                act.wait_ge(ev("mod_full"), k + 1)
                act.copy(mod[:, k // 2, k % 2, :, :].rearrange("p m d -> p (m d)"), four_sc[k]).then_inc(ev("mod_copied"), 1)

            def norm_roots(n, batches=(0, 1)):
                for b in batches:
                    act.wait_ge(ev("var_ready"), 2 * n + b + 1)
                    act.activation(st[:, 3, tiles(b)], st[:, 2, tiles(b)], ACT.Sqrt).then_inc(ev("root_ready"), 1)

            def norm_out(n, batches=(0, 1)):
                layer, m = n // 2, 2 * (n % 2)
                if n == 0:
                    act.wait_ge(ev("modc_ready"), 2)
                for k in [2 * b + half for b in batches for half in range(2)]:
                    act.wait_ge(ev("h_turned"), 4 * n + k + 1)
                    act.activation(hT[:, k * 512:(k + 1) * 512], four_sc[k], ACT.Identity,
                                   scale=modc[:, layer, m + 1, k // 2:k // 2 + 1],
                                   bias=modc[:, layer, m, k // 2:k // 2 + 1]).then_inc(ev("hT_ready"), 1)
                    if n == 2:
                        act.wait_ge(ev("hT_ready"), 4 * n + k + 1)
                        act.wait_ge(ev("x_saved%d" % (k // 2)), 16)
                        act.copy(h_high[:, k * 512:(k + 1) * 512], hT[:, k * 512:(k + 1) * 512]).then_inc(ev("h_high"), 1)

            def norm(n):
                norm_roots(n)
                norm_out(n)

            norm(0)
            for k in range(4):
                act.wait_ge(ev("vec_full"), k + 1)
                act.mul(vec_sb[:, k * 512:(k + 1) * 512], four[k][0:H, :], -1.0).then_inc(ev("vec_ready"), 1)
            act.wait_ge(ev("gates_ready"), 1)
            n_qk = 0
            for f, (kind, b, half) in enumerate(fills0):
                if kind == "v":
                    continue
                act.wait_ge(ev("proj0_full"), f + 1)
                dst, col = (q0T, C_BQ) if kind == "q" else (k0T, C_BK)
                act.activation(dst[:, b * S + half * 512:b * S + half * 512 + 512], four[f % 4], ACT.Identity,
                               bias=cols[:, col:col + 1]).then_inc(ev("qk0_out"), 1)
                n_qk += 1
            for i in range(NT + 2):
                if i < NT:
                    w = (i % TB + 1) * P
                    act.wait_ge(ev("nmax0"), i + 1)
                    if i >= 2:
                        act.wait_ge(ev("pt0B_full"), i - 1)
                    act.activation(probs[:, i % 2, 0:w], SC[i % 2][:, 0:w], ACT.Exp, bias=nmax[:, i % 4:i % 4 + 1],
                                   scale=QK_SCALE, accum_out=rsum[:, i % 8:i % 8 + 1]).then_inc(ev("exp0"), 1)
                if i >= 2:
                    j = i - 2
                    m = min(j % TB + 1, 4)
                    act.wait_ge(ev("pt0A_full"), j + 1)
                    if j >= 4:
                        act.wait_ge(ev("pv0"), j - 3)
                    act.copy(tmp[:, (j % 4) * TB:(j % 4) * TB + m, :].rearrange("p k q -> p (k q)"),
                             PT[0][:, 0:m * P]).then_inc(ev("pt0A_out"), 1)
            norm(1)
            act.wait_ge(ev("logits_shifted"), 1)
            act.activation(rt[:, 1, :, :], rt[:, 0, :, :], ACT.Exp).then_inc(ev("router_exp"), 1)
            for k in range(0, 6, 2):
                act.wait_ge(ev("slots_turned"), k + 1)
                act.copy(slotT[:, k * 512:(k + 1) * 512], four[k % 4]).then_inc(ev("slotT_act"), 1)
            for e in range(E):
                for c in range(FC):
                    act.wait_ge(ev("hidden_full"), e * FC + c + 1)
                    if e >= 2:
                        act.wait_ge(ev("expert_full"), e - 1)
                    act.activation(gelu[:, e % 2, c, 0:CAP], four_sc[c][:, 0:CAP], ACT.Gelu,
                                   bias=cols[:, e * FC + c:e * FC + c + 1]).then_inc(ev("gelu_out"), 1)
            norm_roots(2, (0,))
            norm_out(2, (0,))
            for c in range(6):
                act_chunk(act, 0, c)
                if c == 0:
                    norm_roots(2, (1,))
            norm_out(2, (1,))
            pair_act(act, 0, first=True)
            with act.Fori(1, PAIRS - 1) as p:
                pair_act(act, p)
            pair_act(act, PAIRS - 1, last=True)
            for i in range(STEPS, STEPS + 5):
                act_step(act, PAIRS - 1, i)
            act.wait_ge(ev("ffn_turned"), 1)
            act.copy(wT[:, 0:8, :].rearrange("p w d -> p (w d)"), SC[0][:, :]).then_inc(ev("wT_ready"), 1)
            act.copy(wT[:, 8:13, :].rearrange("p w d -> p (w d)"), SC[1][:, 0:640]).then_inc(ev("wT_ready"), 1)
            norm(3)
            act.wait_ge(ev("logits_shifted"), 2)
            act.activation(rt[:, 1, :, :], rt[:, 0, :, :], ACT.Exp).then_inc(ev("router_exp"), 1)
            for k in range(4):
                act.wait_ge(ev("low_full"), k + 1)
                if k >= 1:
                    act.wait_ge(ev("masked"), 2 * k)
                act.copy(lowrank, MI[:, :]).then_inc(ev("low_ready"), 1)
                for j in range(2):
                    for c in range(FC):
                        n = k * 8 + j * FC + c
                        act.wait_ge(ev("inter_full"), n + 1)
                        if k >= 1 and j == 0 and c == 0:
                            act.wait_ge(ev("y_full"), k)
                        act.activation(act_r[:, j, c, :], four_sc[n % 4], ACT.Relu,
                                       bias=cols[:, C_BI + c:C_BI + c + 1]).then_inc(ev("relu_out"), 1)

        @block.vector
        def _(dve):
            steps = [0]

            def link(ins):
                steps[0] += 1
                ins.then_inc(ev("dve_step"), 1)
                dve.wait_ge(ev("dve_step"), steps[0])

            tt, ts, red = dve.tensor_tensor, dve.tensor_scalar, dve.tensor_reduce
            dve.wait_ge(ev("silu_exp"), 1)
            link(ts(siluT, siluT, 1.0, None, ALU.add))
            link(dve.reciprocal(siluT, siluT))
            tt(siluT, siluT, cols[:, C_C:C_C + 4], ALU.mult).then_inc(ev("silu_ready"), 1)

            def norm_variance(n, b):
                for t in range(b * TB, b * TB + TB):
                    ins = dve.bn_aggr(mv[:, t, :], bst[:, t, :])
                link(ins)
                ts(st[:, 2, tiles(b)], mv[:, tiles(b), 1], EPS, None, ALU.add).then_inc(ev("var_ready"), 1)

            def norm_stats(n, batches=(0, 1)):
                for b in batches:
                    if n == 0:
                        dve.wait_ge(ev("ld_x%d" % b), 16)
                    for t in range(b * TB, b * TB + TB):
                        ins = dve.bn_stats(bst[:, t, :], x[:, t, :])
                    link(ins)
                    norm_variance(n, b)

            def norm_rows(n, batches=(0, 1)):
                for b in batches:
                    dve.wait_ge(ev("var_ready"), 2 * n + b + 1)
                    dve.wait_ge(ev("root_ready"), 2 * n + b + 1)
                    root, var = st[:, 3, tiles(b)], st[:, 2, tiles(b)]
                    link(dve.reciprocal(st[:, 4, tiles(b)], root))
                    link(tt(st[:, 4, tiles(b)], st[:, 4, tiles(b)], var, ALU.mult))
                    link(tt(st[:, 4, tiles(b)], st[:, 4, tiles(b)], root, ALU.add))
                    link(ts(st[:, 4, tiles(b)], st[:, 4, tiles(b)], 0.5, None, ALU.mult))
                    link(dve.reciprocal(st[:, 5, tiles(b)], st[:, 4, tiles(b)]))
                    for t in range(b * TB, b * TB + TB):
                        ins = ts(h[:, t, :], x[:, t, :], mv[:, t, 0:1], st[:, 5, t:t + 1], ALU.subtract, ALU.mult)
                        if t % 4 == 3:
                            ins.then_inc(ev("h_ready"), 1)

            def norm(n):
                norm_stats(n)
                norm_rows(n)

            norm(0)
            dve.wait_ge(ev("modc_full"), 1)
            view = MI[:, 64:64 + 16].rearrange("p (l m b) -> p l m b", l=2, m=4)
            dve.tensor_copy(modc[:, :, 0:4:2, :], view[:, :, 0:4:2, :]).then_inc(ev("modc_ready"), 1)
            ts(modc[:, :, 1:4:2, :], view[:, :, 1:4:2, :], 1.0, None, ALU.add).then_inc(ev("modc_ready"), 1)
            dve.wait_ge(ev("mod_copied"), 4)
            ts(g_pos, gates, 0.0, None, ALU.is_ge)
            ts(g_up, gates, 0.25, None, ALU.max)
            link(ts(g_down, gates, -0.25, None, ALU.min))
            link(tt(g_up, g_up, g_down, ALU.subtract))
            link(tt(g_up, g_up, g_pos, ALU.mult))
            link(tt(gates, g_up, g_down, ALU.add))
            ts(mod[:, 0, :, 2, :], mod[:, 0, :, 2, :], 1.0, None, ALU.add).then_inc(ev("gates_ready"), 1)
            dve.wait_ge(ev("gates_ready"), 1)
            dve.wait_ge(ev("ld_bv"), 16)
            for f, (kind, b, half) in enumerate(fills0):
                if kind != "v":
                    continue
                dve.wait_ge(ev("proj0_full"), f + 1)
                t0 = b * TB + 4 * half
                tt(v0[:, t0:t0 + 4, :], four[f % 4].rearrange("p (t d) -> p t d", d=D), bc_tiles(bvb, 4),
                   ALU.add).then_inc(ev("v0_out"), 1)
            dve.wait_ge(ev("consts"), 8)
            for i in range(NT + 4):
                if i < NT:
                    w = (i % TB + 1) * P
                    dve.wait_ge(ev("scores0"), i + 1)
                    link(tt(SC[i % 2][:, w - P:w], SC[i % 2][:, w - P:w], causal, ALU.add))
                    link(red(st[:, 6, i:i + 1], SC[i % 2][:, 0:w], AX.X, ALU.max))
                    ts(nmax[:, i % 4:i % 4 + 1], st[:, 6, i:i + 1], -QK_SCALE, None, ALU.mult).then_inc(ev("nmax0"), 1)
                if 2 <= i < NT + 2:
                    j = i - 2
                    m = j % TB + 1 - 4
                    dve.wait_ge(ev("pt0B_full"), j + 1)
                    if m > 0:
                        if j >= 4:
                            dve.wait_ge(ev("pv0"), j - 3)
                        dve.tensor_copy(tmp[:, (j % 4) * TB + 4:(j % 4) * TB + 4 + m, :].rearrange("p k q -> p (k q)"),
                                        PT[1][:, 0:m * P]).then_inc(ev("pt0B_out"), 1)
                if i >= 4:
                    j = i - 4
                    dve.wait_ge(ev("pv0"), j + 1)
                    link(dve.reciprocal(rinv[:, j % 4:j % 4 + 1], rsum[:, j % 8:j % 8 + 1]))
                    link(dve.scalar_tensor_tensor(out=Rsb[:, 0, :], in0=CX0[j % 2],
                                                  scalar=rinv[:, j % 4:j % 4 + 1], in1=mod[:, 0, j // TB, 0, :],
                                                  op0=ALU.mult, op1=ALU.mult))
                    ins = tt(x[:, j, :], x[:, j, :], Rsb[:, 0, :], ALU.add)
                    ins.then_inc(ev("att0_out"), 1)
                    dve.wait_ge(ev("att0_out"), j + 1)
            norm(1)

            def router_probs(n):
                lg = MI[:, 0:NT * E].rearrange("p (t e) -> p t e", e=E)
                dve.wait_ge(ev("logits_full"), n + 1)
                if n == 1:
                    dve.wait_ge(ev("ld_ffn"), 16 * 9)
                    link(tt(rt[:, 0, :, :], lg, bc_tiles(gbb, NT), ALU.add))
                else:
                    link(dve.tensor_copy(rt[:, 0, :, :], lg))
                link(red(st[:, 7, :], rt[:, 0, :, :], AX.X, ALU.max))
                tt(rt[:, 0, :, :], rt[:, 0, :, :], bc_rows(st[:, 7, :], E), ALU.subtract).then_inc(ev("logits_shifted"), 1)
                dve.wait_ge(ev("router_exp"), n + 1)
                link(red(st[:, 6, :], rt[:, 1, :, :], AX.X, ALU.add))
                link(dve.reciprocal(st[:, 6, :], st[:, 6, :]))
                link(tt(rt[:, 0, :, :], rt[:, 1, :, :], bc_rows(st[:, 6, :], E), ALU.mult))

            def first_max(best, hot):
                link(red(best, rt[:, 0, :, :], AX.X, ALU.max))
                link(tt(rt[:, 1, :, :], rt[:, 0, :, :], bc_rows(best, E), ALU.is_equal))
                link(tt(rt[:, 1, :, :], rt[:, 1, :, :], bc_tiles(iota8, NT), ALU.mult))
                link(red(st[:, 6, :], rt[:, 1, :, :], AX.X, ALU.min))
                link(tt(hot, bc_tiles(iota8, NT), bc_rows(st[:, 6, :], E), ALU.is_equal))

            router_probs(0)
            first_max(st[:, 7, :], rt[:, 2, :, :])
            dve.tensor_copy(hot1b[:, 1:, :], rt[:, 2, :, :]).then_inc(ev("hot_ready"), 1)
            link(tt(rt[:, 3, :, :], rt[:, 2, :, :], bc_tiles(iota_c, NT), ALU.mult))
            link(red(st[:, 5, :], rt[:, 3, :, :], AX.X, ALU.add))
            dve.wait_ge(ev("ranks_full"), 1)
            link(tt(rt[:, 3, :, :], rt[:, 2, :, :], MI[:, P:2 * P].rearrange("p (t e) -> p t e", e=E), ALU.mult))
            link(red(st[:, 4, :], rt[:, 3, :, :], AX.X, ALU.add))
            link(ts(st[:, 3, :], st[:, 4, :], float(CAP), None, ALU.is_lt))
            link(tt(st[:, 7, :], st[:, 7, :], st[:, 3, :], ALU.mult))
            link(tt(st[:, 6, :], st[:, 4, :], st[:, 5, :], ALU.add))
            link(tt(st[:, 6, :], st[:, 6, :], iota_n, ALU.subtract))
            link(tt(st[:, 6, :], st[:, 6, :], st[:, 3, :], ALU.mult))
            link(tt(slot_s, st[:, 6, :], iota_n, ALU.add))
            link(ts(st[:, 4, :], st[:, 4, :], float(CAP - 1), None, ALU.min))
            tt(slot_g, st[:, 4, :], st[:, 5, :], ALU.add).then_inc(ev("slot_numbers"), 1)
            for k in range(1, 6, 2):
                dve.wait_ge(ev("slots_turned"), k + 1)
                dve.tensor_copy(slotT[:, k * 512:(k + 1) * 512], four[k % 4]).then_inc(ev("slotT_dve"), 1)
            dve.wait_ge(ev("ld_b2"), 16)
            for e in range(E):
                dve.wait_ge(ev("expert_full"), e + 1)
                tt(slot_rows[:, e * CT:(e + 1) * CT, :], PT[e % 2][:, 0:CAP].rearrange("p (t d) -> p t d", d=D),
                   bc_tiles(b2b[:, e, :], CT), ALU.add).then_inc(ev("expert_out"), 1)
            for b in range(B):
                for q in (2 * b, 2 * b + 1):
                    quarter = slice(4 * q, 4 * q + 4)
                    dve.wait_ge(ev("gathered%d" % q), 16 * 4)
                    for t in range(4 * q, 4 * q + 4):
                        ins = dve.scalar_tensor_tensor(out=tmp1[:, t, :], in0=tmp1[:, t, :], scalar=st[:, 7, t:t + 1],
                                                       in1=mod[:, 0, b, 3, :], op0=ALU.mult, op1=ALU.mult)
                    link(ins)
                    ins = tt(x[:, quarter, :], x[:, quarter, :], tmp1[:, quarter, :], ALU.add)
                    ins.then_inc(ev("x_quarter"), 1)
                    dve.wait_ge(ev("x_quarter"), q + 1)
                    for t in range(4 * q, 4 * q + 4):
                        ins = dve.bn_stats(bst[:, t, :], x[:, t, :])
                link(ins)
                norm_variance(2, b)
                if b == 0:
                    norm_rows(2, (0,))
            for c in range(3):
                dve_chunk(dve, 0, c)
            norm_rows(2, (1,))
            for c in range(3, 6):
                dve_chunk(dve, 0, c)
            pair_dve(dve, 0, first=True)
            with dve.Fori(1, PAIRS - 1) as p:
                pair_dve(dve, p)
            pair_dve(dve, PAIRS - 1, last=True)
            for i in range(STEPS, STEPS + 6):
                dve_step(dve, PAIRS - 1, i)
            dve.wait_ge(ev("x_back"), 16)
            for k in range(4):
                dve.wait_ge(ev("wo_full"), k + 1)
                y = tmp1[:, 0:4, :]
                link(tt(y, four[k].rearrange("p (t d) -> p t d", d=D), bc_tiles(mod[:, 1, k // 2, 0, :], 4), ALU.mult))
                link(tt(x[:, 4 * k:4 * k + 4, :], x[:, 4 * k:4 * k + 4, :], y, ALU.add))
            norm(3)
            router_probs(1)
            first_max(st[:, 7, :], rt[:, 2, :, :])
            link(dve.scalar_tensor_tensor(out=rt[:, 0, :, :], in0=rt[:, 2, :, :], scalar=-2.0, in1=rt[:, 0, :, :],
                                          op0=ALU.mult, op1=ALU.add))
            first_max(st[:, 5, :], rt[:, 3, :, :])
            link(tt(rt[:, 3, :, :], rt[:, 3, :, :], rt[:, 2, :, :], ALU.subtract))
            ts(st[:, 4, :], st[:, 5, :], 1.0, None, ALU.mult).then_inc(ev("hot2_ready"), 1)
            dve.wait_ge(ev("hot2_ready"), 1)
            link(tt(st[:, 7, :], st[:, 7, :], st[:, 5, :], ALU.add))
            def write_out(k):
                dve.wait_ge(ev("y_full"), k + 1)
                y = h[:, 4 * k:4 * k + 4, :]
                dve.scalar_tensor_tensor(out=y, in0=bc_tiles(bob, 4), scalar=2.0,
                                         in1=CX[:, :].rearrange("p (t d) -> p t d", d=D), op0=ALU.mult, op1=ALU.add).then_inc(ev("y_out"), 1)
                dve.wait_ge(ev("y_out"), k + 1)
                for t in range(4):
                    ins = dve.scalar_tensor_tensor(out=y[:, t, :], in0=y[:, t, :], scalar=st[:, 7, 4 * k + t:4 * k + t + 1],
                                                   in1=mod[:, 1, k // 2, 3, :], op0=ALU.mult, op1=ALU.mult)
                link(ins)
                tt(x[:, 4 * k:4 * k + 4, :], x[:, 4 * k:4 * k + 4, :], y, ALU.add).then_inc(ev("y_ready"), 1)

            def spread(k):
                for j in range(2):
                    dve.tensor_copy(hot_wide[:, j, :, :].rearrange("p t (e r) -> p t e r", e=E),
                                    rt[:, 2 + j, 4 * k:4 * k + 4, :].unsqueeze(3).to_broadcast([P, 4, E, R])).then_inc(ev("hot_wide"), 1)

            spread(0)
            for k in range(4):
                dve.wait_ge(ev("low_ready"), k + 1)
                for j in range(2):
                    dve.wait_ge(ev("mask_full"), 2 * k + j + 1)
                    if k >= 1:
                        dve.wait_ge(ev("inter_full"), 8 * k)
                    tt(masked[:, j, :], PT[j][:, :], lowrank, ALU.mult).then_inc(ev("masked"), 1)
                if k + 1 < 4:
                    spread(k + 1)
                if k >= 1:
                    write_out(k - 1)
                for c in range(FC):
                    dve.wait_ge(ev("relu_out"), 8 * k + FC + c + 1)
                    tt(act_r[:, 0, c, :], act_r[:, 0, c, :], act_r[:, 1, c, :], ALU.add).then_inc(ev("hidden_sum"), 1)
            write_out(3)

        @block.tensor
        def _(pe):
            mm = pe.matmul

            def keep_clock(bank, n):
                for _ in range(n):
                    mm(bank[:, 0:P], ident[:, :], ident[:, :], start=True, stop=True)

            pe.wait_ge(ev("consts"), 8)
            pe.wait_ge(ev("ld_rows"), 16 * 8)
            pe.transpose(MI[:, 0:NROWS], rows[0:NROWS, :], ident[0:NROWS, 0:NROWS]).then_inc(ev("rows_turned"), 1)
            keep_clock(four[0], 12)
            pe.wait_ge(ev("ld_w0"), 48)
            for n in range(3):
                ins = pe.transpose(SC[0][:, n * P:(n + 1) * P], w0raw[:, n, :], ident[:, :])
            ins.then_inc(ev("w0_turned"), 1)
            pe.wait_ge(ev("w0T_ready"), 1)
            keep_clock(four[0], 5)
            pe.wait_ge(ev("silu_ready"), 1)
            pe.wait_ge(ev("ld_wmod"), 16)
            pe.wait_ge(ev("ld_wmod1"), 16)
            for k in range(4):
                mm(four_sc[k], siluT[:, k:k + 1].to_broadcast([P, P]), wmod[k // 2][:, 2 * D:6 * D],
                   start=True, stop=True).then_inc(ev("mod_full"), 1)
            for layer in range(2):
                for n, m in enumerate((0, 1, 3, 4)):
                    at = 64 + layer * 8 + n * 2
                    ins = mm(MI[:, at:at + 2], wmod[layer][:, m * D:(m + 1) * D], siluT[:, 2 * layer:2 * layer + 2],
                             start=True, stop=True)
            ins.then_inc(ev("modc_full"), 1)

            def norm(n, batches=(0, 1)):
                for k in [2 * b + half for b in batches for half in range(2)]:
                    if k > 0 and n != 2:
                        keep_clock(four_sc[k], 7 if k == 2 else 2)
                    pe.wait_ge(ev("h_ready"), 4 * n + k + 1)
                    for t in range(4):
                        ins = pe.transpose(four_sc[k][:, t * P:(t + 1) * P], h[:, 4 * k + t, :], ident[:, :])
                    ins.then_inc(ev("h_turned"), 1)

            keep_clock(four[0], 12)
            pe.wait_ge(ev("mod_copied"), 4)
            norm(0)
            pe.wait_ge(ev("ld_rel"), 32)
            pe.wait_ge(ev("modc_ready"), 2)
            for k in range(4):
                mm(four[k][0:H, :], rel_sb, hot_sb[:, k * 512:(k + 1) * 512], start=True, stop=True).then_inc(ev("vec_full"), 1)
            pe.wait_ge(ev("vec_ready"), 4)
            for f, (kind, b, half) in enumerate(fills0):
                if f >= 4:
                    name, n = out_of(f - 4)
                    pe.wait_ge(ev(name), n)
                pe.wait_ge(ev("hT_ready"), 2 * b + half + 1)
                at = b * S + half * 512
                if kind == "v":
                    for t in range(4):
                        ins = mm(four[f % 4][:, t * P:(t + 1) * P], hT[:, at + t * P:at + (t + 1) * P], w0T[:, 2, :],
                                 start=True, stop=True)
                else:
                    ins = mm(four[f % 4], w0T[:, "qk".index(kind), :], hT[:, at:at + 512], start=True, stop=True)
                ins.then_inc(ev("proj0_full"), 1)
            pe.wait_ge(ev("qk0_out"), 8)
            pe.wait_ge(ev("v0_out"), 4)
            for i in range(NT + 3):
                if i < NT:
                    b, w = i // TB, (i % TB + 1) * P
                    if i >= 2:
                        pe.wait_ge(ev("exp0"), i - 1)
                    for k in range(0, w, 512):
                        m = min(512, w - k)
                        ins = mm(SC[i % 2][:, k:k + m], q0T[:, i * P:(i + 1) * P], k0T[:, b * S + k:b * S + k + m],
                                 start=True, stop=True)
                    ins.then_inc(ev("scores0"), 1)
                if 2 <= i < NT + 2:
                    j = i - 2
                    pe.wait_ge(ev("exp0"), j + 1)
                    if j >= 1:
                        pe.wait_ge(ev("pt0A_out"), j)
                    nB = sum(1 for a in range(j) if a % TB >= 4)
                    if nB:
                        pe.wait_ge(ev("pt0B_out"), nB)
                    n = j % TB + 1
                    for t in range(n):
                        ins = pe.transpose(PT[t // 4][:, (t % 4) * P:(t % 4) * P + P], probs[:, j % 2, t * P:(t + 1) * P],
                                           ident[:, :])
                        if t == min(n, 4) - 1:
                            ins.then_inc(ev("pt0A_full"), 1)
                            if n <= 4:
                                pe.wait_ge(ev("pt0A_full"), j + 1)
                                pe.sem_inc(ev("pt0B_full"), 1)
                    if n > 4:
                        ins.then_inc(ev("pt0B_full"), 1)
                if i >= 3:
                    j = i - 3
                    pe.wait_ge(ev("pt0A_out"), j + 1)
                    nB = sum(1 for a in range(j + 1) if a % TB >= 4)
                    if nB:
                        pe.wait_ge(ev("pt0B_out"), nB)
                    if j >= 2:
                        pe.wait_ge(ev("att0_out"), j - 1)
                    n = j % TB + 1
                    for t in range(n):
                        ins = mm(CX0[j % 2], tmp[:, (j % 4) * TB + t, :],
                                 v0[:, j // TB * TB + t, :], start=(t == 0), stop=(t == n - 1))
                    ins.then_inc(ev("pv0"), 1)
            keep_clock(four_sc[3], 32)
            norm(1)

            def logits(n, col):
                keep_clock(MI, 4)
                pe.wait_ge(ev("hT_ready"), 4 * (2 * n + 1) + 4)
                for t in range(NT):
                    ins = mm(MI[:, t * E:(t + 1) * E], hT[:, t * P:(t + 1) * P], cols[:, col:col + E], start=True, stop=True)
                ins.then_inc(ev("logits_full"), 1)

            logits(0, C_RW)
            pe.wait_ge(ev("hot_ready"), 1)
            for t in range(NT):
                mm(MI[:, P + t * E:2 * P], ones, hot1b[:, t:t + 1, :].to_broadcast([P, NT - t, E]),
                   start=(t == 0), stop=False, skip_group_check=True)
            ins = mm(MI[:, P:2 * P], before, hot1b[:, 1:, :].rearrange("p t e -> p (t e)"), start=False, stop=True,
                     skip_group_check=True)
            ins.then_inc(ev("ranks_full"), 1)
            pe.wait_ge(ev("scattered"), 16 * NT)
            keep_clock(four_sc[3], 8)
            pe.wait_ge(ev("slots_loaded"), 16)
            pe.wait_ge(ev("slot_numbers"), 1)
            for k in range(6):
                if k >= 4:
                    pe.wait_ge(ev("slotT_act" if k % 2 == 0 else "slotT_dve"), (k - 4) // 2 + 1)
                for t in range(4):
                    ins = pe.transpose(four[k % 4][:, t * P:(t + 1) * P], slot_rows[:, 4 * k + t, :], ident[:, :])
                ins.then_inc(ev("slots_turned"), 1)
            pe.wait_ge(ev("slotT_act"), 3)
            pe.wait_ge(ev("slotT_dve"), 3)
            pe.wait_ge(ev("ld_w1"), 16)
            pe.wait_ge(ev("ld_w2"), 16)
            for e in range(E + 1):
                if e < E:
                    for c in range(FC):
                        if e >= 1:
                            pe.wait_ge(ev("gelu_out"), (e - 1) * FC + c + 1)
                        mm(four_sc[c][:, 0:CAP], w1[:, e, c * P:(c + 1) * P], slotT[:, e * CAP:(e + 1) * CAP],
                           start=True, stop=True).then_inc(ev("hidden_full"), 1)
                if e >= 1:
                    d = e - 1
                    pe.wait_ge(ev("gelu_out"), d * FC + FC)
                    if d >= 2:
                        pe.wait_ge(ev("expert_out"), d - 1)
                    for t in range(CT):
                        for c in range(FC):
                            ins = mm(PT[d % 2][:, t * P:(t + 1) * P], gelu[:, d % 2, c, t * P:(t + 1) * P], w2[:, d, c, :],
                                     start=(c == 0), stop=(c == FC - 1))
                    ins.then_inc(ev("expert_full"), 1)
            pe.wait_ge(ev("gelu_out"), E * FC)
            pe.wait_ge(ev("gathered1"), 16 * 4)
            keep_clock(four_sc[3], 24)
            norm(2, (0,))
            pe.wait_ge(ev("h_split"), 2)
            for c in range(6):
                pe_chunk(pe, 0, c)
            norm(2, (1,))
            pe.wait_ge(ev("h_split"), 4)
            pe.wait_ge(ev("low_out"), 4)
            pe.wait_ge(ev("high_out"), 6)
            pair_pe(pe, 0, first=True)
            with pe.Fori(1, PAIRS - 1) as p:
                pair_pe(pe, p)
            pair_pe(pe, PAIRS - 1, last=True)
            for i in range(STEPS, STEPS + 4):
                pe_step(pe, PAIRS - 1, i)
            pe.wait_ge(ev("ctx_out"), STEPS // 2 * PAIRS)
            pe.wait_ge(ev("ld_wo"), 16)
            for k in range(4):
                for t in range(4):
                    for a in range(PAIRS):
                        lhs = ctxT[:, a, (4 * k + t) * P:(4 * k + t + 1) * P]
                        ins = mm(four[k][:, t * P:(t + 1) * P], lhs, woall[:, a, :], start=(a == 0), stop=(a == PAIRS - 1))
                ins.then_inc(ev("wo_full"), 1)
            pe.wait_ge(ev("ld_ffn"), 16 * 9)
            for n in range(13):
                ins = pe.transpose(SC[n // 8][:, (n % 8) * P:(n % 8) * P + P], raw[:, n, :], ident[:, :])
            ins.then_inc(ev("ffn_turned"), 1)
            pe.wait_ge(ev("wT_ready"), 2)
            keep_clock(four_sc[3], 24)
            norm(3)
            logits(1, C_GW)
            pe.wait_ge(ev("logits_shifted"), 2)
            keep_clock(four_sc[0], 14)

            def choices(k):
                if k >= 1:
                    pe.wait_ge(ev("low_ready"), k)
                mm(MI[:, :], wT[:, LA, :], hT[:, k * 512:(k + 1) * 512], start=True, stop=True).then_inc(ev("low_full"), 1)
                for j in range(2):
                    pe.wait_ge(ev("hot_wide"), 2 * k + j + 1)
                    if k >= 1:
                        pe.wait_ge(ev("masked"), 2 * (k - 1) + j + 1)
                    for t in range(4):
                        ins = pe.transpose(PT[j][:, t * P:(t + 1) * P], hot_wide[:, j, t, :], ident[:, :])
                    ins.then_inc(ev("mask_full"), 1)

            choices(0)
            for k in range(4):
                for j in range(2):
                    for c in range(FC):
                        n = k * 8 + j * FC + c
                        if n >= 4:
                            pe.wait_ge(ev("relu_out"), n - 3)
                        if j == 0:
                            mm(four_sc[c], wT[:, WI + c, :], hT[:, k * 512:(k + 1) * 512], start=True, stop=False,
                               skip_group_check=True)
                        pe.wait_ge(ev("masked"), 2 * k + j + 1)
                        mm(four_sc[c], wT[:, LB + c, :], masked[:, j, :], start=False, stop=True,
                           skip_group_check=True).then_inc(ev("inter_full"), 1)
                if k + 1 < 4:
                    choices(k + 1)
                pe.wait_ge(ev("hidden_sum"), FC * (k + 1))
                if k >= 1:
                    pe.wait_ge(ev("y_out"), k)
                for t in range(4):
                    for c in range(FC):
                        ins = mm(CX[:, t * P:(t + 1) * P], act_r[:, 0, c, t * P:(t + 1) * P], wT[:, WO + c, :],
                                 start=(c == 0), stop=(c == FC - 1))
                ins.then_inc(ev("y_full"), 1)



_INS = ['L0_attn_x', 'L0_attn_Wq', 'L0_attn_bq', 'L0_attn_Wk', 'L0_attn_bk', 'L0_attn_Wv', 'L0_attn_bv',
        'L0_ffn_router_w', 'L0_ffn_w1', 'L0_ffn_b1', 'L0_ffn_w2', 'L0_ffn_b2', 'L0_c', 'L0_wmod',
        'L1_attn_Wq', 'L1_attn_Wk', 'L1_attn_Wv', 'L1_attn_Wo', 'L1_attn_rel_emb',
        'L1_ffn_wi', 'L1_ffn_bi', 'L1_ffn_wo', 'L1_ffn_bo', 'L1_ffn_lora_A', 'L1_ffn_lora_B',
        'L1_ffn_gate_w', 'L1_ffn_gate_b', 'L1_c', 'L1_wmod']


def kernel(**inputs):
    import concourse.bacc as bacc
    from concourse.bass_utils import run_bass_kernel_spmd

    nc = bacc.Bacc("TRN2", target_bir_lowering=False, num_devices=1,
                   dynamic_dma_scratch_size=8192)
    arrays, args = {}, []
    for name in ["rel_hot"] + _INS:
        a = rel_one_hot() if name == "rel_hot" else np.ascontiguousarray(inputs[name])
        arrays["in_" + name] = a
        args.append(nc.dram_tensor("in_" + name, a.shape, mybir.dt.from_np(a.dtype), kind="ExternalInput").ap())
    args.append(nc.dram_tensor("out_0", (B, S, D), F32, kind="ExternalOutput").ap())
    build(nc, *args)
    r = run_bass_kernel_spmd(nc, [arrays], core_ids=[0])
    return r.results[0]["out_0"]
```
